# Optimizing a Trainium2 kernel written in Bass

```python
import numpy as np
import jax
import jax.numpy as jnp

def _softmax(x, axis=-1):
    return jax.nn.softmax(x, axis=axis)

def _gelu(x):
    return jax.nn.gelu(x, approximate=True)

def _silu(x):
    return jax.nn.silu(x)

def _sigmoid(x):
    return jax.nn.sigmoid(x)

def _layernorm(x, axis=-1, eps=1e-05):
    m = jnp.mean(x, axis=axis, keepdims=True)
    v = jnp.var(x, axis=axis, keepdims=True)
    return (x - m) / jnp.sqrt(v + eps)

def _scatter_add(tgt, idx, src, axis=0):
    return tgt.at[idx].add(src)

def _segment_sum(src, seg, n):
    return jax.ops.segment_sum(src, seg, n)
kernel_name = 'mk_gnn_preln_d1_gnn_r64_88fd55'

def setup_inputs(seed: int=0):
    np.random.seed(seed)
    _w = jnp.asarray

    def _rec_inputs():
        import jax
        import jax.numpy as jnp
        _gk = jax.random.key(seed)
        x = -0.0003713 + 1 * jax.random.normal(jax.random.fold_in(_gk, 1), (50000, 256), jnp.float32)
        src = jax.random.randint(jax.random.fold_in(_gk, 2), (12500,), 0, 50000, jnp.int32)
        dst = jnp.minimum((50000 * jax.random.uniform(jax.random.fold_in(_gk, 3), (12500,)) ** 2.0).astype(jnp.int32), 49999)
        _o = jnp.argsort(dst, stable=True)
        src = src[_o]
        dst = dst[_o]
        return (x, src, dst)
    x, src, dst = _rec_inputs()

    def _L0_gnn_setup():
        import jax, jax.numpy as jnp
        import numpy as np
        N, E = (50000, 12500)
        IN_DIM = 256
        OUT_DIM = 256
        H = 8
        D = OUT_DIM // H
        SCALE = D ** (-0.5)
        LN_EPS = 1e-05

        def _layernorm(x, g, b):
            mu = jnp.mean(x, axis=-1, keepdims=True)
            var = jnp.mean((x - mu) ** 2, axis=-1, keepdims=True)
            return (x - mu) * jax.lax.rsqrt(var + LN_EPS) * g + b
        key = jax.random.key(seed)
        ks = jax.random.split(key, 12)
        s = 1.0 / np.sqrt(IN_DIM)
        inp = {'x': jax.random.normal(ks[0], (N, IN_DIM), jnp.float32), 'edge_index': jax.random.randint(ks[1], (2, E), 0, N, jnp.int64), 'batch': jnp.zeros((N,), jnp.int64), 'Wq': jax.random.uniform(ks[2], (IN_DIM, OUT_DIM), jnp.float32, -s, s), 'Wk': jax.random.uniform(ks[3], (IN_DIM, OUT_DIM), jnp.float32, -s, s), 'Wv': jax.random.uniform(ks[4], (IN_DIM, OUT_DIM), jnp.float32, -s, s), 'Wo_w': jax.random.uniform(ks[5], (OUT_DIM, OUT_DIM), jnp.float32, -s, s), 'Wo_b': jnp.zeros((OUT_DIM,), jnp.float32), 'ln1_g': jnp.ones((OUT_DIM,), jnp.float32), 'ln1_b': jnp.zeros((OUT_DIM,), jnp.float32), 'ln2_g': jnp.ones((OUT_DIM,), jnp.float32), 'ln2_b': jnp.zeros((OUT_DIM,), jnp.float32), 'ffn_w1': jax.random.uniform(ks[6], (OUT_DIM, 2 * OUT_DIM), jnp.float32, -s, s), 'ffn_b1': jnp.zeros((2 * OUT_DIM,), jnp.float32), 'ffn_w2': jax.random.uniform(ks[7], (2 * OUT_DIM, OUT_DIM), jnp.float32, -s, s), 'ffn_b2': jnp.zeros((OUT_DIM,), jnp.float32)}
        return inp
    _L0_gnn_all = _L0_gnn_setup()
    _L0_gnn_in = {k: v for k, v in _L0_gnn_all.items() if k in ('Wq', 'Wk', 'Wv', 'Wo_w', 'Wo_b', 'ln1_g', 'ln1_b', 'ln2_g', 'ln2_b', 'ffn_w1', 'ffn_b1', 'ffn_w2', 'ffn_b2')}
    del _L0_gnn_all
    return {'x': x, 'src': src, 'dst': dst, 'L0_gnn_Wq': _L0_gnn_in['Wq'], 'L0_gnn_Wk': _L0_gnn_in['Wk'], 'L0_gnn_Wv': _L0_gnn_in['Wv'], 'L0_gnn_Wo_w': _L0_gnn_in['Wo_w'], 'L0_gnn_Wo_b': _L0_gnn_in['Wo_b'], 'L0_gnn_ln1_g': _L0_gnn_in['ln1_g'], 'L0_gnn_ln1_b': _L0_gnn_in['ln1_b'], 'L0_gnn_ln2_g': _L0_gnn_in['ln2_g'], 'L0_gnn_ln2_b': _L0_gnn_in['ln2_b'], 'L0_gnn_ffn_w1': _L0_gnn_in['ffn_w1'], 'L0_gnn_ffn_b1': _L0_gnn_in['ffn_b1'], 'L0_gnn_ffn_w2': _L0_gnn_in['ffn_w2'], 'L0_gnn_ffn_b2': _L0_gnn_in['ffn_b2']}

def reference(x, src, dst, L0_gnn_Wq, L0_gnn_Wk, L0_gnn_Wv, L0_gnn_Wo_w, L0_gnn_Wo_b, L0_gnn_ln1_g, L0_gnn_ln1_b, L0_gnn_ln2_g, L0_gnn_ln2_b, L0_gnn_ffn_w1, L0_gnn_ffn_b1, L0_gnn_ffn_w2, L0_gnn_ffn_b2):
    import jax
    import jax.numpy as jnp

    def _L0_gnn_ref(x, edge_index, batch, Wq, Wk, Wv, Wo_w, Wo_b, ln1_g, ln1_b, ln2_g, ln2_b, ffn_w1, ffn_b1, ffn_w2, ffn_b2):
        import jax, jax.numpy as jnp
        import numpy as np
        N, E = (50000, 12500)
        IN_DIM = 256
        OUT_DIM = 256
        H = 8
        D = OUT_DIM // H
        SCALE = D ** (-0.5)
        LN_EPS = 1e-05

        def _layernorm(x, g, b):
            mu = jnp.mean(x, axis=-1, keepdims=True)
            var = jnp.mean((x - mu) ** 2, axis=-1, keepdims=True)
            return (x - mu) * jax.lax.rsqrt(var + LN_EPS) * g + b
        n = x.shape[0]
        residual = x
        Q = (x @ Wq).reshape(n, H, D)
        K = (x @ Wk).reshape(n, H, D)
        V = (x @ Wv).reshape(n, H, D)
        src, dst = (edge_index[0], edge_index[1])
        scores = jnp.einsum('ehd,ehd->eh', Q[dst], K[src]) * SCALE
        attn_max = jnp.zeros((n, H), scores.dtype).at[dst].max(scores)
        w = jnp.exp(scores - attn_max[dst])
        attn_sum = jnp.zeros((n, H), w.dtype).at[dst].add(w)
        w = w / (attn_sum[dst] + 1e-08)
        msg = V[src] * w[:, :, None]
        out = jnp.zeros((n, H, D), msg.dtype).at[dst].add(msg)
        out = out.reshape(n, OUT_DIM) @ Wo_w + Wo_b
        out = _layernorm(residual + out, ln1_g, ln1_b)
        ffn = jax.nn.gelu(out @ ffn_w1 + ffn_b1, approximate=False) @ ffn_w2 + ffn_b2
        out = _layernorm(out + ffn, ln2_g, ln2_b)
        return out
    edge_index = jnp.stack([src, dst])
    batch0 = jnp.zeros((50000,), jnp.int32)
    h = jnp.maximum(_layernorm(x, axis=-1), 0.0)
    x = x + _L0_gnn_ref(h, edge_index, batch0, L0_gnn_Wq, L0_gnn_Wk, L0_gnn_Wv, L0_gnn_Wo_w, L0_gnn_Wo_b, L0_gnn_ln1_g, L0_gnn_ln1_b, L0_gnn_ln2_g, L0_gnn_ln2_b, L0_gnn_ffn_w1, L0_gnn_ffn_b1, L0_gnn_ffn_w2, L0_gnn_ffn_b2)
    return x

_drawn_inputs = setup_inputs


def setup_inputs(seed=0):
    import zlib

    import numpy as np

    out = dict(_drawn_inputs(seed))
    spreads = {'L0_gnn_Wo_b': (0.0, 0.1),
     'L0_gnn_ln1_g': (1.0, 0.2),
     'L0_gnn_ln1_b': (0.0, 0.1),
     'L0_gnn_ln2_g': (1.0, 0.2),
     'L0_gnn_ln2_b': (0.0, 0.1),
     'L0_gnn_ffn_b1': (0.0, 0.309),
     'L0_gnn_ffn_b2': (0.0, 0.1)}
    factors = {'L0_gnn_Wq': 8.0, 'L0_gnn_Wk': 8.0}
    for name, (base, spread) in spreads.items():
        noise = np.random.default_rng([zlib.crc32(name.encode()), seed]).standard_normal(out[name].shape)
        drawn = base * np.exp(spread * noise) if base else spread * noise
        out[name] = jnp.asarray(drawn.astype(out[name].dtype))
    for name, factor in factors.items():
        out[name] = (out[name] * factor).astype(out[name].dtype)
    return out
```

```python
import numpy as np
import concourse.bass as bass
from concourse import mybir
from contextlib import ExitStack

N, E, D, H, F = 50000, 12500, 256, 8, 512
P = 128
KD = D // P
KF = F // P
HD = D // H
SCALE = HD ** -0.5
LN_EPS = 1e-5
SUM_EPS = 1e-8
GT = 4
GR = GT * P
EG = -(-E // GR)
EP = EG * GR
SC = P // H
SE = EP // SC
NG = -(-N // GR)
NFILL = 7
FR = -(-N // (P * NFILL))
NP = P * NFILL * FR
SKIP = 1 << 17

f32 = mybir.dt.float32
f32r = mybir.dt.float32r
i32 = mybir.dt.int32
ACT = mybir.ActivationFunctionType
ALU = mybir.AluOpType
AX = mybir.AxisListType


class Step:

    def __init__(self, c, i=None, unroll=1):
        self.c, self.i, self.unroll = c, i, unroll

    def __add__(self, d):
        return Step(self.c + d, self.i, self.unroll)

    def exists(self, n):
        return self.i is not None or 0 <= self.c < n

    def times(self, k, extra=0):
        return k * self.c + extra if self.i is None else self.i * (k * self.unroll) + (k * self.c + extra)

    def after(self, k):
        assert self.i is None or self.c >= k
        return self.c >= k

    def use(self, ring, k=1, extra=0):
        c = self.c // ring + 1
        return k * c + extra if self.i is None else self.i * (k * (self.unroll // ring)) + (k * c + extra)


def pipeline(engine, first, last, lo, hi, unroll, body):
    for c in range(first, lo):
        body(Step(c))
    with engine.Fori(0, (hi - lo) // unroll) as i:
        for k in range(unroll):
            body(Step(lo + k, i, unroll))
    for c in range(hi, last):
        body(Step(c))


def hold(engine, semaphore, value, passed):
    engine.wait_ge(semaphore, value)
    engine.sem_inc(passed, 1)


def score_stage(nc, x, ends_cols, wq, wk, wv, wo_b, vt, score_dram, agg_dram):
    with ExitStack() as ctx:
        def sb(name, shape, dt=f32):
            return ctx.enter_context(nc.sbuf_tensor(name, shape, dt))

        def sem(name):
            return ctx.enter_context(nc.semaphore(name))

        ident = sb("a_ident", [P, P])
        head_of = sb("a_head_of", [P, KD, H])
        idx = sb("a_idx", [P, EG * 2 * GT], i32)
        idx_now = [sb(f"a_idx_now{r}", [P, 2 * GT], i32) for r in range(2)]
        w_raw = [sb(f"a_w{n}_raw", [P, KD, D]) for n in "qkv"]
        w_hi = [sb(f"a_w{n}_hi", [P, KD, D], f32r) for n in "qkv"]
        w_lo = [sb(f"a_w{n}_lo", [P, KD, D], f32r) for n in "qkv"]
        bias_row = sb("a_bias_row", [P, D])
        xg = [[sb(f"a_x{n}{r}", [P, GT, D]) for r in range(2)] for n in ("d", "s")]
        stats = sb("a_stats", [P, 2, 2, GT, 6])
        mv = sb("a_mv", [P, 2, 2, GT, 2])
        veps = sb("a_veps", [P, 2, 2, GT])
        rstd = sb("a_rstd", [P, 2, 2, GT])
        nmean = sb("a_nmean", [P, 2, 2, GT])
        nmr = sb("a_nmr", [P, 2, 2, GT])
        mhalf = sb("a_mhalf", [P, 2, GT])
        h = [[sb(f"a_h{n}{r}", [P, GT, D]) for r in range(2)] for n in ("d", "s")]
        ht_hi = [sb(f"a_ht{n}_hi", [P, KD, GR], f32r) for n in ("d", "s")]
        ht_lo = [sb(f"a_ht{n}_lo", [P, KD, GR], f32r) for n in ("d", "s")]
        ksb = sb("a_ksb", [P, KD, GR])
        prod = sb("a_prod", [P, KD, GR])
        score = [sb(f"a_score{r}", [H, GR]) for r in range(2)]
        T = ctx.enter_context(nc.psum_tensor("a_T", [P, KD, GR], f32))
        Q = ctx.enter_context(nc.psum_tensor("a_Q", [P, KD, GR], f32))
        K = ctx.enter_context(nc.psum_tensor("a_K", [P, KD, GR], f32))
        V0 = ctx.enter_context(nc.psum_tensor("a_V0", [P, GR], f32))
        S = ctx.enter_context(nc.psum_tensor("a_S", [P, GR], f32))
        V = [V0[:, :], K[:, 0, :]]

        idx_in, idx_set, w_in, bias_in, filled = sem("a_idx_in"), sem("a_idx_set"), sem("a_w_in"), sem("a_bias_in"), sem("a_filled")
        gathered = [[sem(f"a_gathered_{n}{r}") for r in range(2)] for n in ("d", "s")]
        consts, w_split, w_hi_done = sem("a_consts"), sem("a_w_split"), sem("a_w_hi_done")
        stats_done, mv_done, veps_done, rstd_done, nmr_done = (
            sem("a_stats_done"), sem("a_mv_done"), sem("a_veps_done"), sem("a_rstd_done"), sem("a_nmr_done"))
        h_done = [sem("a_hd_done"), sem("a_hs_done")]
        t_done = [sem("a_td_done"), sem("a_ts_done")]
        hi_done = [sem("a_hid_done"), sem("a_his_done")]
        lo_done = [sem("a_lod_done"), sem("a_los_done")]
        q_done, k_done, v_done = sem("a_q_done"), sem("a_k_done"), sem("a_v_done")
        k_out, v_out, prod_done = sem("a_k_out"), sem("a_v_out"), sem("a_prod_done")
        s_done, s_out = sem("a_s_done"), sem("a_s_out")
        stored = [sem(f"a_stored{r}") for r in range(2)]
        passed, pool_passed = sem("a_passed"), sem("a_pool_passed")
        FIRST, LO, HI = -3, 2, EG - 3
        with nc.Block() as block:
            @block.sync
            def _(sp):
                sp.dma_start(idx[:], ends_cols).then_inc(idx_in, 16)
                for raw, w in zip(w_raw, (wq, wk, wv)):
                    sp.dma_start(raw[:], w.rearrange("(k p) n -> p k n", p=P)).then_inc(w_in, 16)

                def step(s):
                    if s.exists(EG):
                        sp.wait_ge(s_out, s.times(1, 1))
                        sp.dma_start(score_dram[:, bass.ds(s.times(GR), GR)], score[s.c % 2][:])\
                          .then_inc(stored[s.c % 2], 16)
                pipeline(sp, 0, EG, LO, HI, 2, step)
                for r in range(2):
                    sp.wait_ge(stored[r], 16 * ((EG + 1 - r) // 2))
                sp.wait_ge(filled, 16 * NFILL)

            @block.gpsimd
            def _(pool):
                nc.gpsimd.memset(ident[:], 0.0).then_inc(consts, 1)
                nc.gpsimd.memset(head_of[:], 1.0).then_inc(consts, 1)
                nc.gpsimd.memset(mhalf[:], -0.5).then_inc(consts, 1)
                pool.wait_ge(consts, 3)
                nc.gpsimd.affine_select(out=ident[:], in_=ident[:], compare_op=ALU.not_equal, fill=1.0, base=0,
                                        pattern=[[-1, P]], channel_multiplier=1).then_inc(consts, 1)
                nc.gpsimd.affine_select(out=head_of[:], in_=head_of[:], compare_op=ALU.is_ge, fill=0.0, base=0,
                                        pattern=[[P, KD], [-HD, H]], channel_multiplier=1).then_inc(consts, 1)
                pool.wait_ge(consts, 5)
                nc.gpsimd.affine_select(out=head_of[:], in_=head_of[:], compare_op=ALU.is_ge, fill=0.0, base=HD - 1,
                                        pattern=[[-P, KD], [HD, H]], channel_multiplier=-1).then_inc(consts, 1)
                pool.wait_ge(idx_in, 16)

                def step(s):
                    g = s + 3
                    if g.exists(EG):
                        r = g.c % 2
                        for side in range(2):
                            if g.after(2):
                                pool.wait_ge(h_done[side], g.times(1, -1))
                        nc.gpsimd.tensor_copy(idx_now[r][:], idx[:, bass.ds(g.times(2 * GT), 2 * GT)]).then_inc(idx_set, 1)
                        hold(pool, idx_set, g.times(1, 1), pool_passed)
                        for side in range(2):
                            for j in range(GT):
                                nc.gpsimd.indirect_dma_start(
                                    xg[side][r][:, j, :], None, x,
                                    bass.IndirectOffsetOnAxis(idx_now[r][:, side * GT + j:side * GT + j + 1], 0),
                                ).then_inc(gathered[side][r], 16)
                    g = s + 2
                    if g.exists(EG):
                        r = g.c % 2
                        hold(pool, mv_done, g.times(1, 1), pool_passed)
                        nc.gpsimd.tensor_scalar(nmean[:, r], mv[:, r, :, :, 0], -1.0, 0.0, ALU.mult, ALU.add)
                        nc.gpsimd.tensor_scalar(veps[:, r], mv[:, r, :, :, 1], 1.0, LN_EPS, ALU.mult, ALU.add)\
                            .then_inc(veps_done, 1)
                        pool.wait_ge(veps_done, g.times(1, 1))
                        nc.gpsimd.tensor_tensor(rstd[:, r], veps[:, r], mhalf[:], ALU.pow).then_inc(rstd_done, 1)
                        pool.wait_ge(rstd_done, g.times(1, 1))
                        nc.gpsimd.tensor_tensor(nmr[:, r], nmean[:, r], rstd[:, r], ALU.mult)\
                            .then_inc(nmr_done, 1)
                pipeline(pool, FIRST, EG, LO, HI, 2, step)

            @block.vector
            def _(dve):
                dve.wait_ge(w_in, 48)
                for n in range(3):
                    nc.vector.tensor_copy(w_hi[n][:], w_raw[n][:]).then_inc(w_hi_done, 1)
                for n in range(3):
                    dve.wait_ge(w_hi_done, n + 1)
                    nc.vector.tensor_tensor(w_lo[n][:], w_raw[n][:], w_hi[n][:].bitcast(f32), ALU.subtract)\
                        .then_inc(w_split, 1)

                def step(s):
                    g = s + 2
                    if g.exists(EG):
                        r = g.c % 2
                        if g.after(2):
                            dve.wait_ge(nmr_done, g.times(1, -1))
                        for side in range(2):
                            dve.wait_ge(gathered[side][r], g.use(2, 16 * GT))
                            for j in range(GT):
                                nc.vector.bn_stats(stats[:, r, side, j, :], xg[side][r][:, j, :]).then_inc(stats_done, 1)
                        for side in range(2):
                            hold(dve, stats_done, g.times(2 * GT, (side + 1) * GT), passed)
                            for j in range(GT):
                                ins = nc.vector.bn_aggr(mv[:, r, side, j, :], stats[:, r, side, j, :])
                        ins.then_inc(mv_done, 1)
                    if s.exists(EG):
                        for c in range(KD):
                            dve.wait_ge(q_done, s.times(KD, c + 1))
                            dve.wait_ge(k_out, s.times(KD, c + 1))
                            if s.after(1):
                                dve.wait_ge(s_done, s.times(1))
                            nc.vector.tensor_tensor(prod[:, c, :], Q[:, c, :], ksb[:, c, :], ALU.mult)\
                                .then_inc(prod_done, 1)
                    g = s + 1
                    if g.exists(EG):
                        for side in range(2):
                            for c in range(KD):
                                dve.wait_ge(hi_done[side], g.times(KD, c + 1))
                                nc.vector.tensor_tensor(ht_lo[side][:, c, :], T[:, c, :],
                                                        ht_hi[side][:, c, :].bitcast(f32), ALU.subtract)\
                                    .then_inc(lo_done[side], 1)
                pipeline(dve, FIRST, EG, LO, HI, 2, step)

            @block.scalar
            def _(act):
                act.dma_start(bias_row[:], wo_b.broadcast_to([P, D])).then_inc(bias_in, 16)
                act.wait_ge(bias_in, 16)
                table = agg_dram.rearrange("(n p r) d -> n p r d", n=NFILL, p=P)
                for n in range(NFILL):
                    act.dma_start(table[n], bias_row[:].rearrange("p (r d) -> p r d", r=1)
                                  .broadcast_to([P, FR, D])).then_inc(filled, 16)

                def step(s):
                    if s.exists(EG):
                        for c in range(KD):
                            act.wait_ge(k_done, s.times(KD, c + 1))
                            if s.after(1):
                                act.wait_ge(prod_done, s.times(KD, c - 1))
                            nc.scalar.copy(ksb[:, c, :], K[:, c, :]).then_inc(k_out, 1)
                    g = s + 1

                    def high_part(side):
                        for c in range(KD):
                            act.wait_ge(t_done[side], g.times(1, 1))
                            nc.scalar.copy(ht_hi[side][:, c, :], T[:, c, :]).then_inc(hi_done[side], 1)
                    if g.exists(EG):
                        high_part(0)
                    if s.exists(EG):
                        for c in range(KD):
                            act.wait_ge(v_done, s.times(KD, c + 1))
                            nc.scalar.copy(vt[:, c, bass.ds(s.times(GR), GR)], V[c]).then_inc(v_out, 1)
                    if g.exists(EG):
                        high_part(1)
                    if s.exists(EG):
                        act.wait_ge(s_done, s.times(1, 1))
                        if s.after(2):
                            act.wait_ge(stored[s.c % 2], (s + -2).use(2, 16))
                        nc.scalar.mul(score[s.c % 2][:], S[0:H, :], SCALE).then_inc(s_out, 1)
                    g = s + 2
                    if g.exists(EG):
                        r = g.c % 2
                        act.wait_ge(nmr_done, g.times(1, 1))
                        act.wait_ge(rstd_done, g.times(1, 1))
                        for side in range(2):
                            if g.after(2):
                                act.wait_ge(t_done[side], g.times(1, -1))
                            act.wait_ge(gathered[side][r], g.use(2, 16 * GT))
                            for j in range(GT):
                                ins = nc.scalar.activation(h[side][r][:, j, :], xg[side][r][:, j, :], ACT.Relu,
                                                           bias=nmr[:, r, side, j:j + 1], scale=rstd[:, r, side, j:j + 1])
                            ins.then_inc(h_done[side], 1)
                pipeline(act, FIRST, EG, LO, HI, 2, step)

            @block.tensor
            def _(pe):
                pe.wait_ge(consts, 6)
                pe.wait_ge(w_split, 3)

                def project(out, n, side, c):
                    for k in range(KD):
                        for p, (w, a) in enumerate(((w_hi, ht_hi), (w_hi, ht_lo), (w_lo, ht_hi))):
                            ins = nc.tensor.matmul(out, w[n][:, k, c * P:(c + 1) * P], a[side][:, k, :],
                                                   start=(k == 0 and p == 0), stop=(k == KD - 1 and p == 2))
                    return ins

                def transpose(g, side):
                    pe.wait_ge(h_done[side], g.times(1, 1))
                    if side == 1:
                        pe.wait_ge(lo_done[0], g.times(KD, KD))
                    elif g.after(1):
                        pe.wait_ge(lo_done[1], g.times(KD))
                    for j in range(GT):
                        for k in range(KD):
                            ins = nc.tensor.transpose(T[:, k, j * P:(j + 1) * P],
                                                      h[side][g.c % 2][:, j, k * P:(k + 1) * P], ident[:])
                    ins.then_inc(t_done[side], 1)

                def step(s):
                    g = s + 1
                    if s.exists(EG):
                        pe.wait_ge(lo_done[0], s.times(KD, KD))
                        if s.after(1):
                            pe.wait_ge(prod_done, s.times(KD))
                        for c in range(KD):
                            project(Q[:, c, :], 0, 0, c).then_inc(q_done, 1)
                        pe.wait_ge(lo_done[1], s.times(KD, KD))
                        if s.after(1):
                            pe.wait_ge(v_out, s.times(KD))
                        for c in range(KD):
                            project(K[:, c, :], 1, 1, c).then_inc(k_done, 1)
                    if g.exists(EG):
                        transpose(g, 0)
                    if s.exists(EG):
                        project(V[0], 2, 1, 0).then_inc(v_done, 1)
                        pe.wait_ge(k_out, s.times(KD, 1))
                        project(V[1], 2, 1, 1).then_inc(v_done, 1)
                    if g.exists(EG):
                        transpose(g, 1)
                    if s.exists(EG):
                        pe.wait_ge(prod_done, s.times(KD, KD))
                        if s.after(1):
                            pe.wait_ge(s_out, s.times(1))
                        for k in range(KD):
                            ins = nc.tensor.matmul(S[0:H, :], head_of[:, k, :], prod[:, k, :],
                                                   start=(k == 0), stop=(k == KD - 1))
                        ins.then_inc(s_done, 1)
                pipeline(pe, FIRST, EG, LO, HI, 2, step)


def softmax_stage(nc, dst_windows, score_dram, alpha_dram, cont_dram):
    with ExitStack() as ctx:
        def sb(name, shape, dt=f32):
            return ctx.enter_context(nc.sbuf_tensor(name, shape, dt))

        def sem(name):
            return ctx.enter_context(nc.semaphore(name))

        dst = sb("b_dst", [P, SE + 2], i32)
        cont = sb("b_cont", [P, SE + 1])
        score, fwd, run = sb("b_score", [P, SE]), sb("b_fwd", [P, SE]), sb("b_run", [P, SE])
        weight = sb("b_weight", [P, SE])
        ident = sb("b_ident", [P, P])
        one = sb("b_one", [1, 1])
        ends = sb("b_ends", [P, 2])
        rows = sb("b_rows", [1, 2, P])
        carry = sb("b_carry", [1, P + 1])
        carry_col = sb("b_carry_col", [P, 1])
        row_ps = ctx.enter_context(nc.psum_tensor("b_row_ps", [P, 2, P], f32))
        col_ps = ctx.enter_context(nc.psum_tensor("b_col_ps", [P, 512], f32))
        loaded, consts, dve_done, rows_done, col_done, exp_done, stored = (
            sem("b_loaded"), sem("b_consts"), sem("b_dve_done"), sem("b_rows_done"), sem("b_col_done"),
            sem("b_exp_done"), sem("b_stored"))
        marks = {}
        with nc.Block() as block:
            @block.gpsimd
            def _(pool):
                nc.gpsimd.memset(ident[:], 0.0).then_inc(consts, 1)
                nc.gpsimd.memset(one[:], 1.0).then_inc(consts, 1)
                pool.wait_ge(consts, 2)
                nc.gpsimd.affine_select(out=ident[:], in_=ident[:], compare_op=ALU.not_equal, fill=1.0, base=0,
                                        pattern=[[-1, P]], channel_multiplier=1).then_inc(consts, 1)

            @block.vector
            def _(dve):
                n = [0]

                def done(ins):
                    n[0] += 1
                    ins.then_inc(dve_done, 1)
                    dve.wait_ge(dve_done, n[0])

                dve.wait_ge(loaded, 32)
                done(nc.vector.tensor_tensor(cont[:], dst[:, 1:SE + 2], dst[:, 0:SE + 1], ALU.is_equal))
                marks["cont"] = n[0]
                done(nc.vector.tensor_reduce(ends[:, 0:1], cont[:, 0:SE], AX.X, ALU.min))
                done(nc.vector.tensor_reduce(ends[:, 1:2], cont[:, 1:SE + 1], AX.X, ALU.min))

                def scan(number, out, values, op, back):
                    turn = slice(None, None, -1) if back else slice(None)
                    flags = (cont[:, 1:SE + 1] if back else cont[:, 0:SE])[:, turn]
                    done(nc.vector.tensor_tensor_scan(out[:, turn], flags, values[:, turn], 0.0, ALU.mult, op))
                    marks["scan", number] = n[0]
                    dve.wait_ge(rows_done, number + 1)
                    done(nc.vector.tensor_copy(rows[:], row_ps[0:1, :, :]))
                    done(nc.vector.memset(carry[:, P:P + 1] if back else carry[:, 0:1], 0.0))
                    to = carry[:, 0:P] if back else carry[:, 1:P + 1]
                    done(nc.vector.tensor_tensor_scan(to[:, turn], rows[:, 1, turn], rows[:, 0, turn], 0.0,
                                                      ALU.mult, op))
                    marks["carry", number] = n[0]
                    dve.wait_ge(col_done, number + 1)
                    done(nc.vector.tensor_copy(carry_col[:], col_ps[:, 0:1]))
                    done(nc.vector.tensor_tensor_scan(out[:, turn], flags, values[:, turn], carry_col[:], ALU.mult, op))

                scan(0, fwd, score, ALU.max, False)
                scan(1, run, fwd, ALU.max, True)
                done(nc.vector.tensor_tensor(score[:], score[:], run[:], ALU.subtract))
                marks["shifted"] = n[0]
                dve.wait_ge(exp_done, 1)
                scan(2, fwd, weight, ALU.add, False)
                scan(3, run, fwd, ALU.max, True)
                done(nc.vector.tensor_scalar(run[:], run[:], SUM_EPS, None, ALU.add))
                done(nc.vector.reciprocal(fwd[:], run[:]))
                done(nc.vector.tensor_tensor(weight[:], weight[:], fwd[:], ALU.mult))
                marks["alpha"] = n[0]

            @block.scalar
            def _(act):
                act.wait_ge(dve_done, marks["shifted"])
                nc.scalar.activation(weight[:], score[:], ACT.Exp).then_inc(exp_done, 1)

            @block.tensor
            def _(pe):
                pe.wait_ge(consts, 3)
                for number, (out, back) in enumerate(((fwd, 0), (run, 1), (fwd, 0), (run, 1))):
                    last = out[:, 0:1] if back else out[:, SE - 1:SE]
                    pe.wait_ge(dve_done, marks["scan", number])
                    nc.tensor.matmul(row_ps[0:1, 0, :], last, ident[:], start=True, stop=True)
                    nc.tensor.matmul(row_ps[0:1, 1, :], ends[:, back:back + 1], ident[:], start=True, stop=True)\
                        .then_inc(rows_done, 1)
                    pe.wait_ge(dve_done, marks["carry", number])
                    nc.tensor.matmul(col_ps[:, 0:1], carry[0:1, back:back + P], one[:], start=True, stop=True)\
                        .then_inc(col_done, 1)

            @block.sync
            def _(sp):
                sp.dma_start(score[:], score_dram.rearrange("h (c e) -> (h c) e", c=SC)).then_inc(loaded, 16)
                sp.dma_start(dst[:], dst_windows).then_inc(loaded, 16)
                sp.wait_ge(dve_done, marks["cont"])
                sp.dma_start(cont_dram.rearrange("o (c e) -> (o c) e", c=SC), cont[0:SC, 0:SE]).then_inc(stored, 16)
                sp.wait_ge(dve_done, marks["alpha"])
                sp.dma_start(alpha_dram.rearrange("h (c e) -> (h c) e", c=SC), weight[:]).then_inc(stored, 16)
                sp.wait_ge(stored, 32)


def message_stage(nc, dst_cols, next_cols, wo, wo_b, vt, alpha_dram, cont_dram, agg_dram):
    with ExitStack() as ctx:
        def sb(name, shape, dt=f32):
            return ctx.enter_context(nc.sbuf_tensor(name, shape, dt))

        def sem(name):
            return ctx.enter_context(nc.semaphore(name))

        spread = sb("c_spread", [H, KD, P])
        dst, nxt = sb("c_dst", [P, EG * GT], i32), sb("c_next", [P, EG * GT], i32)
        same, row_of = sb("c_same", [P, EG * GT]), sb("c_row_of", [P, EG * GT], i32)
        row_now = [sb(f"c_row_now{r}", [P, GT], i32) for r in range(2)]
        w = sb("c_wo", [P, KD, D])
        bias_row = sb("c_bias_row", [P, D])
        alpha = [sb(f"c_alpha{r}", [H, GR]) for r in range(2)]
        cont = [sb(f"c_cont{r}", [P, GR]) for r in range(2)]
        msg = [sb(f"c_msg{r}", [P, KD, GR]) for r in range(2)]
        total = [sb(f"c_total{r}", [P, KD, GR]) for r in range(2)]
        rows = [sb(f"c_rows{r}", [P, GT, D]) for r in range(2)]
        A = [ctx.enter_context(nc.psum_tensor(f"c_A{r}", [P, KD, GR], f32)) for r in range(2)]
        Y = [ctx.enter_context(nc.psum_tensor(f"c_Y{r}", [P, GT, D], f32)) for r in range(2)]
        loaded, consts, same_done, index_done = sem("c_loaded"), sem("c_consts"), sem("c_same_done"), sem("c_index_done")
        group_in = [sem(f"c_group_in{r}") for r in range(2)]
        a_done, msg_done, total_done, y_done, rows_done = (
            sem("c_a_done"), sem("c_msg_done"), sem("c_total_done"), sem("c_y_done"), sem("c_rows_done"))
        scattered = [sem(f"c_scattered{r}") for r in range(2)]
        row_set, passed = sem("c_row_set"), sem("c_passed")
        FIRST, LO, HI = -1, 3, EG - 2
        with nc.Block() as block:
            @block.sync
            def _(sp):
                sp.dma_start(dst[:], dst_cols).then_inc(loaded, 16)
                sp.dma_start(nxt[:], next_cols).then_inc(loaded, 16)
                sp.dma_start(w[:], wo.rearrange("(k p) n -> p k n", p=P)).then_inc(loaded, 16)
                sp.dma_start(bias_row[:], wo_b.broadcast_to([P, D])).then_inc(loaded, 16)

                def step(s):
                    g = s + 1
                    if g.exists(EG):
                        r = g.c % 2
                        if g.after(2):
                            sp.wait_ge(total_done, g.times(KD, -KD))
                        sp.dma_start(alpha[r][:], alpha_dram[:, bass.ds(g.times(GR), GR)]).then_inc(group_in[r], 16)
                        sp.dma_start(cont[r][:], cont_dram[:, bass.ds(g.times(GR), GR)].broadcast_to([P, GR]))\
                          .then_inc(group_in[r], 16)
                pipeline(sp, FIRST, EG, LO, HI, 2, step)

            @block.tensor
            def _(pe):
                pe.wait_ge(consts, 3)
                pe.wait_ge(loaded, 64)

                def step(s):
                    g = s + 1
                    if g.exists(EG):
                        r = g.c % 2
                        pe.wait_ge(group_in[r], g.use(2, 32))
                        if g.after(2):
                            pe.wait_ge(msg_done, g.times(KD, -KD))
                        for c in range(KD):
                            nc.tensor.matmul(A[r][:, c, :], spread[:, c, :], alpha[r][:], start=True, stop=True)\
                                .then_inc(a_done, 1)
                    if s.exists(EG):
                        r = s.c % 2
                        pe.wait_ge(total_done, s.times(KD, KD))
                        if s.after(2):
                            pe.wait_ge(rows_done, s.times(1, -1))
                        for j in range(GT):
                            for k in range(KD):
                                ins = nc.tensor.matmul(Y[r][:, j, :], total[r][:, k, j * P:(j + 1) * P], w[:, k, :],
                                                       start=(k == 0), stop=(k == KD - 1))
                        ins.then_inc(y_done, 1)
                pipeline(pe, FIRST, EG, LO, HI, 2, step)

            @block.vector
            def _(dve):
                dve.wait_ge(loaded, 64)
                nc.vector.tensor_tensor(same[:], dst[:], nxt[:], ALU.is_equal).then_inc(same_done, 1)
                dve.wait_ge(same_done, 1)
                nc.vector.scalar_tensor_tensor(row_of[:], same[:], float(SKIP), dst[:], ALU.mult, ALU.add)\
                    .then_inc(index_done, 1)

                def step(s):
                    if s.exists(EG):
                        r = s.c % 2
                        dve.wait_ge(group_in[r], s.use(2, 32))
                        if s.after(2):
                            dve.wait_ge(y_done, s.times(1, -1))
                        for c in range(KD):
                            dve.wait_ge(a_done, s.times(KD, c + 1))
                            nc.vector.tensor_tensor(msg[r][:, c, :], A[r][:, c, :],
                                                    vt[:, c, bass.ds(s.times(GR), GR)], ALU.mult).then_inc(msg_done, 1)
                        for c in range(KD):
                            dve.wait_ge(msg_done, s.times(KD, c + 1))
                            if s.after(1):
                                dve.wait_ge(total_done, s.times(KD, c - 1))
                            before = total[1 - r][:, c, GR - 1:GR] if s.after(1) else 0.0
                            nc.vector.tensor_tensor_scan(total[r][:, c, :], cont[r][:], msg[r][:, c, :], before,
                                                         ALU.mult, ALU.add).then_inc(total_done, 1)
                    g = s + -1
                    if g.exists(EG):
                        r = g.c % 2
                        dve.wait_ge(y_done, g.times(1, 1))
                        if g.after(2):
                            dve.wait_ge(scattered[r], (g + -2).use(2, 16 * GT))
                        nc.vector.tensor_tensor(rows[r][:], Y[r][:], bias_row[:].rearrange("p (j d) -> p j d", j=1)
                                                .broadcast_to([P, GT, D]), ALU.add).then_inc(rows_done, 1)
                pipeline(dve, 0, EG + 1, LO, HI, 2, step)

            @block.gpsimd
            def _(pool):
                nc.gpsimd.memset(spread[:], 1.0).then_inc(consts, 1)
                pool.wait_ge(consts, 1)
                nc.gpsimd.affine_select(out=spread[:], in_=spread[:], compare_op=ALU.is_ge, fill=0.0, base=0,
                                        pattern=[[P, KD], [1, P]], channel_multiplier=-HD).then_inc(consts, 1)
                pool.wait_ge(consts, 2)
                nc.gpsimd.affine_select(out=spread[:], in_=spread[:], compare_op=ALU.is_ge, fill=0.0, base=HD - 1,
                                        pattern=[[-P, KD], [-1, P]], channel_multiplier=HD).then_inc(consts, 1)
                pool.wait_ge(index_done, 1)

                def step(s):
                    if s.exists(EG):
                        r = s.c % 2
                        pool.wait_ge(rows_done, s.times(1, 1))
                        nc.gpsimd.tensor_copy(row_now[r][:], row_of[:, bass.ds(s.times(GT), GT)]).then_inc(row_set, 1)
                        hold(pool, row_set, s.times(1, 1), passed)
                        for j in range(GT):
                            nc.gpsimd.indirect_dma_start(
                                agg_dram, bass.IndirectOffsetOnAxis(row_now[r][:, j:j + 1], 0),
                                rows[r][:, j, :], None, bounds_check=N - 1, oob_is_err=False,
                            ).then_inc(scattered[r], 16)
                pipeline(pool, 0, EG, LO, HI, 2, step)
                for r in range(2):
                    pool.wait_ge(scattered[r], 16 * GT * ((EG + 1 - r) // 2))


def node_stage(nc, x, wo_cols, w1, w2, out, agg_dram):
    with ExitStack() as ctx:
        def sb(name, shape, dt=f32):
            return ctx.enter_context(nc.sbuf_tensor(name, shape, dt))

        def sem(name):
            return ctx.enter_context(nc.semaphore(name))

        def psum(name, shape):
            return ctx.enter_context(nc.psum_tensor(name, shape, f32))

        w1_raw, w2_raw = sb("d_w1_raw", [P, KD, F]), sb("d_w2_raw", [P, KF, D])
        w1_hi, w1_lo = sb("d_w1_hi", [P, KD, F], f32r), sb("d_w1_lo", [P, KD, F], f32r)
        w2_hi, w2_lo = sb("d_w2_hi", [P, KF, D], f32r), sb("d_w2_lo", [P, KF, D], f32r)
        g1_col, b1_col, fb1_col = sb("d_g1_col", [P, KD]), sb("d_b1_col", [P, KD]), sb("d_fb1_col", [P, KF])
        g1_row, g2_row, b2_row = sb("d_g1_row", [P, D]), sb("d_g2_row", [P, D]), sb("d_b2_row", [P, D])
        res_row = sb("d_res_row", [1, 4, D])
        res_hi = sb("d_res_hi", [1, D], f32r)
        res = sb("d_res", [P, 2, D], f32r)
        ones = sb("d_ones", [P, P], f32r)
        ones_f = sb("d_ones_f", [P, P])
        zero_f = sb("d_zero_f", [P, 2 * D])
        ident = sb("d_ident", [P, P])
        mhalf = sb("d_mhalf", [P, GT])
        xt = [sb(f"d_x{r}", [P, GT, D]) for r in range(4)]
        xb = [sb(f"d_xb{r}", [P, GT, D]) for r in range(4)]
        agg = [sb(f"d_agg{r}", [P, GT, D]) for r in range(2)]
        h = [sb(f"d_h{r}", [P, GT, D]) for r in range(2)]
        z = sb("d_z", [P, GT, D])
        zn = [sb(f"d_zn{r}", [P, GT, D]) for r in range(2)]
        zt_hi, zt_lo = sb("d_zt_hi", [P, KD, GR], f32r), sb("d_zt_lo", [P, KD, GR], f32r)
        act_full = sb("d_act", [P, KF, GR])
        act_hi, act_lo = sb("d_act_hi", [P, KF, GR], f32r), sb("d_act_lo", [P, KF, GR], f32r)
        u = sb("d_u", [P, GT, D])
        y = [sb(f"d_y{r}", [P, GT, D]) for r in range(2)]
        yn = sb("d_yn", [P, GT, D])
        o = [sb(f"d_o{r}", [P, GT, D]) for r in range(2)]
        norm = {n: dict(stats=sb(f"d_stats_{n}", [P, 2, GT, 6]), mv=sb(f"d_mv_{n}", [P, 2, GT, 2]),
                        veps=sb(f"d_veps_{n}", [P, 2, GT]), rstd=sb(f"d_rstd_{n}", [P, 2, GT]),
                        nmean=sb(f"d_nmean_{n}", [P, 2, GT]), nmr=sb(f"d_nmr_{n}", [P, 2, GT]), stats_done=sem(f"d_stats_done_{n}"),
                        mv_done=sem(f"d_mv_done_{n}"), veps_done=sem(f"d_veps_done_{n}"),
                        rstd_done=sem(f"d_rstd_done_{n}"), nmr_done=sem(f"d_nmr_done_{n}")) for n in "xzy"}
        T, FF, Y = psum("d_T", [P, KD, GR]), psum("d_F", [P, KF, GR]), psum("d_Y", [P, GT, D])

        w_in, consts, prep, bias_ps = sem("d_w_in"), sem("d_consts"), sem("d_prep"), sem("d_bias_ps")
        x_in = [sem(f"d_x_in{r}") for r in range(4)]
        agg_in = [sem(f"d_agg_in{r}") for r in range(2)]
        stored = [sem(f"d_stored{r}") for r in range(2)]
        h_done, z_done, zn_done, xb_done, u_done = (
            sem("d_h_done"), sem("d_z_done"), sem("d_zn_done"), sem("d_xb_done"), sem("d_u_done"))
        t_done, hi_done, lo_done = sem("d_t_done"), sem("d_hi_done"), sem("d_lo_done")
        f_done, gelu_done, ghi_done, glo_done = sem("d_f_done"), sem("d_gelu_done"), sem("d_ghi_done"), sem("d_glo_done")
        ffn_done, y_done, yn_done, scaled, o_done = (
            sem("d_ffn_done"), sem("d_y_done"), sem("d_yn_done"), sem("d_scaled"), sem("d_o_done"))
        passed, pool_passed = sem("d_passed"), sem("d_pool_passed")
        v = wo_cols
        vectors = ((g1_col, v["g1_col"]), (b1_col, v["b1_col"]), (fb1_col, v["fb1_col"]),
                   (g1_row, v["g1"].broadcast_to([P, D])), (g2_row, v["g2"].broadcast_to([P, D])),
                   (b2_row, v["b2"].broadcast_to([P, D])),
                   (res_row[:, 0, :], v["b1"]), (res_row[:, 1, :], v["fb2"]))
        N_IN = 16 * (2 + len(vectors))
        FIRST, LO, HI, LAST = -4, 5, NG - 5, NG + 2
        PREP = 13

        def wide(row):
            return row[:].rearrange("p (j d) -> p j d", j=1).broadcast_to([P, GT, D])

        def rows_of(table, g):
            at = g.times(GR) if g.i is not None or g.c < NG - 1 else N - GR
            return table[bass.ds(at, GR), :].rearrange("(p j) d -> p j d", j=GT)

        with nc.Block() as block:
            @block.sync
            def _(sp):
                sp.dma_start(w1_raw[:], w1.rearrange("(k p) n -> p k n", p=P)).then_inc(w_in, 16)
                sp.dma_start(w2_raw[:], w2.rearrange("(k p) n -> p k n", p=P)).then_inc(w_in, 16)
                for to, of in vectors:
                    sp.dma_start(to[:], of).then_inc(w_in, 16)

                def step(s):
                    g = s + 4
                    if g.exists(NG):
                        if g.after(4):
                            sp.wait_ge(xb_done, g.times(1, -3))
                            sp.wait_ge(h_done, g.times(1, -3))
                        sp.dma_start(xt[g.c % 4][:], rows_of(x, g)).then_inc(x_in[g.c % 4], 16)
                    g = s + 3
                    if g.exists(NG):
                        if g.after(2):
                            sp.wait_ge(z_done, g.times(1, -1))
                        sp.dma_start(agg[g.c % 2][:], rows_of(agg_dram, g)).then_inc(agg_in[g.c % 2], 16)
                    g = s + -2
                    if g.exists(NG):
                        sp.wait_ge(o_done, g.times(1, 1))
                        if g.i is None and g.c == NG - 1:
                            sp.wait_ge(stored[(g.c - 1) % 2], (g + -1).use(2, 16))
                        sp.dma_start(rows_of(out, g), o[g.c % 2][:]).then_inc(stored[g.c % 2], 16)
                pipeline(sp, FIRST, LAST, LO, HI, 4, step)
                for r in range(2):
                    sp.wait_ge(stored[r], 16 * ((NG + 1 - r) // 2))

            @block.gpsimd
            def _(pool):
                nc.gpsimd.memset(ident[:], 0.0).then_inc(consts, 1)
                nc.gpsimd.memset(mhalf[:], -0.5).then_inc(consts, 1)
                nc.gpsimd.memset(ones_f[:], 1.0).then_inc(consts, 1)
                nc.gpsimd.memset(zero_f[:], 0.0).then_inc(consts, 1)
                pool.wait_ge(consts, 4)
                nc.gpsimd.affine_select(out=ident[:], in_=ident[:], compare_op=ALU.not_equal, fill=1.0, base=0,
                                        pattern=[[-1, P]], channel_multiplier=1).then_inc(consts, 1)
                pool.wait_ge(w_in, N_IN)

                def scales(n, g):
                    q, r = norm[n], g.c % 2
                    hold(pool, q["mv_done"], g.times(1, 1), pool_passed)
                    nc.gpsimd.tensor_scalar(q["nmean"][:, r], q["mv"][:, r, :, 0], -1.0, 0.0, ALU.mult, ALU.add)
                    nc.gpsimd.tensor_scalar(q["veps"][:, r], q["mv"][:, r, :, 1], 1.0, LN_EPS, ALU.mult, ALU.add)\
                        .then_inc(q["veps_done"], 1)
                    pool.wait_ge(q["veps_done"], g.times(1, 1))
                    nc.gpsimd.tensor_tensor(q["rstd"][:, r], q["veps"][:, r], mhalf[:], ALU.pow)\
                        .then_inc(q["rstd_done"], 1)
                    pool.wait_ge(q["rstd_done"], g.times(1, 1))
                    nc.gpsimd.tensor_tensor(q["nmr"][:, r], q["nmean"][:, r], q["rstd"][:, r], ALU.mult)\
                        .then_inc(q["nmr_done"], 1)

                def step(s):
                    g = s + 1
                    if g.exists(NG):
                        scales("z", g)
                    g = s + -2
                    if g.exists(NG):
                        pool.wait_ge(yn_done, g.times(1, 1))
                        if g.after(2):
                            pool.wait_ge(stored[g.c % 2], (g + -2).use(2, 16))
                        nc.gpsimd.tensor_tensor(o[g.c % 2][:], yn[:], wide(g2_row), ALU.mult).then_inc(scaled, 1)
                    g = s + -1
                    if g.exists(NG):
                        scales("y", g)
                    if s.exists(NG):
                        pool.wait_ge(zn_done, s.times(1, 1))
                        if s.after(1):
                            pool.wait_ge(y_done, s.times(1))
                        nc.gpsimd.tensor_tensor(u[:], zn[s.c % 2][:], wide(g1_row), ALU.mult).then_inc(u_done, 1)
                    g = s + 3
                    if g.exists(NG):
                        scales("x", g)
                    g = s + 1
                    if g.exists(NG):
                        pool.wait_ge(x_in[g.c % 4], g.use(4, 16))
                        if g.after(4):
                            pool.wait_ge(o_done, g.times(1, -3))
                        nc.gpsimd.tensor_tensor(xb[g.c % 4][:], xt[g.c % 4][:], wide(b2_row), ALU.add)\
                            .then_inc(xb_done, 1)
                pipeline(pool, FIRST, LAST, LO, HI, 4, step)

            @block.vector
            def _(dve):
                n = [0]

                def done(ins):
                    n[0] += 1
                    ins.then_inc(prep, 1)
                    dve.wait_ge(prep, n[0])

                dve.wait_ge(w_in, N_IN)
                dve.wait_ge(consts, 5)
                dve.wait_ge(bias_ps, 1)
                done(nc.vector.tensor_tensor(fb1_col[:], fb1_col[:], FF[:, 0, 0:KF], ALU.add))
                for k in range(KD):
                    done(nc.vector.tensor_scalar(w1_raw[:, k, :], w1_raw[:, k, :], g1_col[:, k:k + 1], None, ALU.mult))
                done(nc.vector.tensor_copy(w1_hi[:], w1_raw[:]))
                done(nc.vector.tensor_tensor(w1_lo[:], w1_raw[:], w1_hi[:].bitcast(f32), ALU.subtract))
                done(nc.vector.tensor_copy(w2_hi[:], w2_raw[:]))
                done(nc.vector.tensor_tensor(w2_lo[:], w2_raw[:], w2_hi[:].bitcast(f32), ALU.subtract))
                done(nc.vector.tensor_copy(ones[:], ones_f[:]))
                done(nc.vector.tensor_copy(res[:].rearrange("p a d -> p (a d)"), zero_f[:]))
                done(nc.vector.tensor_tensor(res_row[:, 2, :], res_row[:, 0, :], res_row[:, 1, :], ALU.add))
                done(nc.vector.tensor_copy(res_hi[:], res_row[:, 2, :]))
                done(nc.vector.tensor_tensor(res_row[:, 3, :], res_row[:, 2, :], res_hi[:].bitcast(f32), ALU.subtract))
                for a in range(2):
                    nc.vector.tensor_copy(res[0:1, a, :], res_row[:, 2, :]).then_inc(prep, 1)
                    nc.vector.tensor_copy(res[32:33, a, :], res_row[:, 3, :]).then_inc(prep, 1)

                def statistics(name, g, t):
                    q, r = norm[name], g.c % 2
                    for j in range(GT):
                        nc.vector.bn_stats(q["stats"][:, r, j, :], t[:, j, :]).then_inc(q["stats_done"], 1)
                    hold(dve, q["stats_done"], g.times(GT, GT), passed)
                    for j in range(GT):
                        ins = nc.vector.bn_aggr(q["mv"][:, r, j, :], q["stats"][:, r, j, :])
                    ins.then_inc(q["mv_done"], 1)

                def low_part(s, c):
                    dve.wait_ge(ghi_done, s.times(KF, c + 1))
                    nc.vector.tensor_tensor(act_lo[:, c, :], act_full[:, c, :], act_hi[:, c, :].bitcast(f32),
                                            ALU.subtract).then_inc(glo_done, 1)

                def step(s):
                    g = s + -1
                    if g.exists(NG):
                        dve.wait_ge(ffn_done, g.times(1, 1))
                        dve.wait_ge(u_done, g.times(1, 1))
                        if g.after(2):
                            dve.wait_ge(yn_done, g.times(1, -1))
                        nc.vector.tensor_tensor(y[g.c % 2][:], Y[:], u[:], ALU.add).then_inc(y_done, 1)
                        dve.wait_ge(y_done, g.times(1, 1))
                        statistics("y", g, y[g.c % 2])
                    if s.exists(NG):
                        low_part(s, 0)
                        low_part(s, 1)
                    g = s + 3
                    if g.exists(NG):
                        dve.wait_ge(x_in[g.c % 4], g.use(4, 16))
                        statistics("x", g, xt[g.c % 4])
                    g = s + -2
                    if g.exists(NG):
                        r = g.c % 2
                        dve.wait_ge(scaled, g.times(1, 1))
                        dve.wait_ge(xb_done, g.times(1, 1))
                        nc.vector.tensor_tensor(o[r][:], o[r][:], xb[g.c % 4][:], ALU.add).then_inc(o_done, 1)
                    if s.exists(NG):
                        low_part(s, 2)
                        low_part(s, 3)
                    g = s + 1
                    if g.exists(NG):
                        dve.wait_ge(hi_done, g.times(1, 1))
                        nc.vector.tensor_tensor(zt_lo[:], T[:], zt_hi[:].bitcast(f32), ALU.subtract).then_inc(lo_done, 1)
                    g = s + 2
                    if g.exists(NG):
                        r = g.c % 2
                        dve.wait_ge(h_done, g.times(1, 1))
                        dve.wait_ge(agg_in[r], g.use(2, 16))
                        if g.after(1):
                            dve.wait_ge(zn_done, g.times(1))
                        nc.vector.tensor_tensor(z[:], h[r][:], agg[r][:], ALU.add).then_inc(z_done, 1)
                        dve.wait_ge(z_done, g.times(1, 1))
                        statistics("z", g, z)
                pipeline(dve, FIRST, LAST, LO, HI, 4, step)

            @block.scalar
            def _(act):
                act.wait_ge(prep, 1)

                def normalize(name, g, to, of, j, func=ACT.Identity):
                    q, r = norm[name], g.c % 2
                    return nc.scalar.activation(to[:, j, :], of[:, j, :], func, bias=q["nmr"][:, r, j:j + 1],
                                                scale=q["rstd"][:, r, j:j + 1])

                def gelu(s, c):
                    act.wait_ge(f_done, s.times(KF, c + 1))
                    if s.after(1):
                        act.wait_ge(glo_done, s.times(KF, c + 1 - KF))
                    nc.scalar.activation(act_full[:, c, :], FF[:, c, :], ACT.Gelu, bias=fb1_col[:, c:c + 1])\
                        .then_inc(gelu_done, 1)
                    act.wait_ge(gelu_done, s.times(KF, c + 1))
                    nc.scalar.activation(act_hi[:, c, :], act_full[:, c, :], ACT.Identity).then_inc(ghi_done, 1)

                def step(s):
                    g = s + 1
                    r = g.c % 2

                    def norm_z(tiles):
                        if g.exists(NG):
                            if 0 in tiles:
                                act.wait_ge(norm["z"]["nmr_done"], g.times(1, 1))
                                if g.after(2):
                                    act.wait_ge(t_done, g.times(1, -1))
                                    act.wait_ge(u_done, g.times(1, -1))
                            for j in tiles:
                                ins = normalize("z", g, zn[r], z, j)
                            if GT - 1 in tiles:
                                ins.then_inc(zn_done, 1)
                    norm_z((0, 1))
                    if s.exists(NG):
                        gelu(s, 0)
                    norm_z((2,))
                    if s.exists(NG):
                        gelu(s, 1)
                    norm_z((3,))
                    if s.exists(NG):
                        gelu(s, 2)
                        gelu(s, 3)
                    if g.exists(NG):
                        act.wait_ge(t_done, g.times(1, 1))
                        nc.scalar.activation(zt_hi[:], T[:], ACT.Identity).then_inc(hi_done, 1)
                    g2 = s + -1
                    if g2.exists(NG):
                        act.wait_ge(norm["y"]["nmr_done"], g2.times(1, 1))
                        if g2.after(1):
                            act.wait_ge(scaled, g2.times(1))
                        for j in range(GT):
                            ins = normalize("y", g2, yn, y[g2.c % 2], j)
                        ins.then_inc(yn_done, 1)
                    g3 = s + 3
                    if g3.exists(NG):
                        act.wait_ge(norm["x"]["nmr_done"], g3.times(1, 1))
                        if g3.after(2):
                            act.wait_ge(z_done, g3.times(1, -1))
                        for j in range(GT):
                            ins = normalize("x", g3, h[g3.c % 2], xt[g3.c % 4], j, ACT.Relu)
                        ins.then_inc(h_done, 1)
                pipeline(act, FIRST, LAST, LO, HI, 4, step)

            @block.tensor
            def _(pe):
                pe.wait_ge(w_in, N_IN)
                for c in range(KF):
                    for k in range(KD):
                        ins = nc.tensor.matmul(FF[:, 0, c:c + 1], w1_raw[:, k, c * P:(c + 1) * P], b1_col[:, k:k + 1],
                                               start=(k == 0), stop=(k == KD - 1))
                ins.then_inc(bias_ps, 1)
                pe.wait_ge(prep, PREP + 2)

                def step(s):
                    if s.exists(NG):
                        pe.wait_ge(lo_done, s.times(1, 1))
                        for c in range(KF):
                            if s.after(1):
                                pe.wait_ge(gelu_done, s.times(KF, c + 1 - KF))
                            for k in range(KD):
                                for p, (w, a) in enumerate(((w1_hi, zt_hi), (w1_hi, zt_lo), (w1_lo, zt_hi))):
                                    ins = nc.tensor.matmul(FF[:, c, :], w[:, k, c * P:(c + 1) * P], a[:, k, :],
                                                           start=(k == 0 and p == 0), stop=(k == KD - 1 and p == 2))
                            ins.then_inc(f_done, 1)
                    g = s + 1
                    if g.exists(NG):
                        pe.wait_ge(zn_done, g.times(1, 1))
                        if g.after(1):
                            pe.wait_ge(lo_done, g.times(1))
                        for j in range(GT):
                            for k in range(KD):
                                ins = nc.tensor.transpose(T[:, k, j * P:(j + 1) * P],
                                                          zn[g.c % 2][:, j, k * P:(k + 1) * P], ident[:])
                        ins.then_inc(t_done, 1)
                    if s.exists(NG):
                        if s.after(1):
                            pe.wait_ge(y_done, s.times(1))
                        for b in range(GT // 2):
                            nc.tensor.matmul(Y[:, 2 * b:2 * b + 2, :], ones[:], res[:], start=True, stop=False,
                                             skip_group_check=True)
                        for c in range(KF):
                            pe.wait_ge(glo_done, s.times(KF, c + 1))
                            for j in range(GT):
                                for a, w in ((act_hi, w2_hi), (act_lo, w2_hi), (act_hi, w2_lo)):
                                    ins = nc.tensor.matmul(Y[:, j, :], a[:, c, j * P:(j + 1) * P], w[:, c, :],
                                                           start=False, stop=(c == KF - 1 and w is w2_lo),
                                                           skip_group_check=True)
                        ins.then_inc(ffn_done, 1)
                pipeline(pe, FIRST, LAST, LO, HI, 4, step)


def program(nc, x, ends_cols, dst_row_cols, next_cols, dst_windows, wq, wk, wv, wo, wo_b, g1, b1, g2, b2,
            g1_col, b1_col, fb1_col, fb2, w1, w2, out):
    with ExitStack() as ctx:
        score_dram = nc.dram_tensor("score_scratch", [H, EP], f32).ap()
        alpha_dram = nc.dram_tensor("alpha_scratch", [H, EP], f32).ap()
        cont_dram = nc.dram_tensor("cont_scratch", [1, EP], f32).ap()
        agg_dram = nc.dram_tensor("agg_scratch", [NP, D], f32).ap()
        with nc.sbuf_tensor("vt", [P, KD, EP], f32) as vt:
            score_stage(nc, x, ends_cols, wq, wk, wv, wo_b, vt, score_dram, agg_dram)
            softmax_stage(nc, dst_windows, score_dram, alpha_dram, cont_dram)
            message_stage(nc, dst_row_cols, next_cols, wo, wo_b, vt, alpha_dram, cont_dram, agg_dram)
        vectors = dict(g1=g1, b1=b1, g2=g2, b2=b2, g1_col=g1_col, b1_col=b1_col, fb1_col=fb1_col, fb2=fb2)
        node_stage(nc, x, vectors, w1, w2, out, agg_dram)


def kernel(**inputs):
    import numpy as _np
    import concourse.bacc as _bacc
    from concourse import mybir as _mybir
    from concourse.bass_utils import run_bass_kernel_spmd as _run

    given = {k: _np.asarray(v) for k, v in inputs.items()}
    src, dst = given["src"], given["dst"]

    def columns(a, fill):
        padded = _np.full(EP, fill, a.dtype)
        padded[:E] = a
        return padded.reshape(EG, GT, P).transpose(2, 0, 1)

    ext = _np.full(EP + 2, N, dst.dtype)
    ext[0], ext[-1] = -1, N + 1
    ext[1:E + 1] = dst
    windows = _np.stack([ext[c * SE:c * SE + SE + 2] for c in range(SC)])
    L = "L0_gnn_"
    arrays = dict(
        x=given["x"], ends_cols=_np.stack([columns(dst, 0), columns(src, 0)], axis=2).reshape(P, -1),
        dst_row_cols=_np.ascontiguousarray(ext[1:-1].reshape(EG * GT, P).T),
        next_cols=_np.ascontiguousarray(ext[2:].reshape(EG * GT, P).T),
        dst_windows=_np.ascontiguousarray(_np.concatenate([windows] * H)),
        wq=given[L + "Wq"], wk=given[L + "Wk"], wv=given[L + "Wv"], wo=given[L + "Wo_w"],
        wo_b=given[L + "Wo_b"].reshape(1, D), g1=given[L + "ln1_g"].reshape(1, D), b1=given[L + "ln1_b"].reshape(1, D),
        g2=given[L + "ln2_g"].reshape(1, D), b2=given[L + "ln2_b"].reshape(1, D),
        g1_col=_np.ascontiguousarray(given[L + "ln1_g"].reshape(KD, P).T),
        b1_col=_np.ascontiguousarray(given[L + "ln1_b"].reshape(KD, P).T),
        fb1_col=_np.ascontiguousarray(given[L + "ffn_b1"].reshape(KF, P).T),
        fb2=given[L + "ffn_b2"].reshape(1, D), w1=given[L + "ffn_w1"], w2=given[L + "ffn_w2"])
    nc = _bacc.Bacc("TRN2", target_bir_lowering=False, num_devices=1)
    args, host = {}, {}
    for name, a in arrays.items():
        a = _np.ascontiguousarray(a)
        host[f"in_{name}"] = a
        args[name] = nc.dram_tensor(f"in_{name}", a.shape, _mybir.dt.from_np(a.dtype), kind="ExternalInput").ap()
    args["out"] = nc.dram_tensor("out_0", (N, D), _mybir.dt.float32, kind="ExternalOutput").ap()
    program(nc, **args)
    r = _run(nc, [host], core_ids=[0])
    return r.results[0]["out_0"]
```

```python
import numpy as np
import concourse.bass as bass
from concourse import mybir
from contextlib import ExitStack

N, E, D, H, F = 50000, 12500, 256, 8, 512
P = 128
KD = D // P
KF = F // P
HD = D // H
SCALE = HD ** -0.5
LN_EPS = 1e-5
SUM_EPS = 1e-8
GT = 4
GR = GT * P
EG = -(-E // GR)
EP = EG * GR
SC = P // H
SE = EP // SC
NG = -(-N // GR)
NFILL = 2 * EG
FR = -(-N // (P * NFILL))
NP = P * NFILL * FR
SKIP = 1 << 17

f32 = mybir.dt.float32
f32r = mybir.dt.float32r
i32 = mybir.dt.int32
ACT = mybir.ActivationFunctionType
ALU = mybir.AluOpType
AX = mybir.AxisListType


class Step:

    def __init__(self, c, i=None, unroll=1):
        self.c, self.i, self.unroll = c, i, unroll

    def __add__(self, d):
        return Step(self.c + d, self.i, self.unroll)

    def exists(self, n):
        return self.i is not None or 0 <= self.c < n

    def times(self, k, extra=0):
        return k * self.c + extra if self.i is None else self.i * (k * self.unroll) + (k * self.c + extra)

    def after(self, k):
        assert self.i is None or self.c >= k
        return self.c >= k

    def use(self, ring, k=1, extra=0):
        c = self.c // ring + 1
        return k * c + extra if self.i is None else self.i * (k * (self.unroll // ring)) + (k * c + extra)


def pipeline(engine, first, last, lo, hi, unroll, body):
    for c in range(first, lo):
        body(Step(c))
    with engine.Fori(0, (hi - lo) // unroll) as i:
        for k in range(unroll):
            body(Step(lo + k, i, unroll))
    for c in range(hi, last):
        body(Step(c))


def hold(engine, semaphore, value, passed):
    engine.wait_ge(semaphore, value)
    engine.sem_inc(passed, 1)


def score_stage(nc, x, ends_cols, wq, wk, wv, wo_b, vt, score_dram, agg_dram):
    with ExitStack() as ctx:
        def sb(name, shape, dt=f32):
            return ctx.enter_context(nc.sbuf_tensor(name, shape, dt))

        def sem(name):
            return ctx.enter_context(nc.semaphore(name))

        ident = sb("a_ident", [P, P])
        head_of = sb("a_head_of", [P, KD, H])
        idx = sb("a_idx", [P, EG * 2 * GT], i32)
        idx_now = [sb(f"a_idx_now{r}", [P, 2 * GT], i32) for r in range(4)]
        w_hi = [sb(f"a_w{n}_hi", [P, KD, D], f32r) for n in "qkv"]
        w_lo = [sb(f"a_w{n}_lo", [P, KD, D], f32r) for n in "qkv"]
        bias_row = sb("a_bias_row", [P, D])
        xg = [[sb(f"a_x{n}{r}", [P, GT, D]) for r in range(4)] for n in ("d", "s")]
        stats = sb("a_stats", [P, 2, 2, GT, 6])
        mv = sb("a_mv", [P, 2, 2, GT, 2])
        veps = sb("a_veps", [P, 2, 2, GT])
        rstd = sb("a_rstd", [P, 2, 2, GT])
        nmean = sb("a_nmean", [P, 2, 2, GT])
        nmr = sb("a_nmr", [P, 2, 2, GT])
        mhalf = sb("a_mhalf", [P, 2, GT])
        h = [sb(f"a_h{n}", [P, GT, D]) for n in ("d", "s")]
        w_raw = [h[0][:, 0:KD, :], h[0][:, KD:2 * KD, :], h[1][:, 0:KD, :]]
        ht_hi = [sb(f"a_ht{n}_hi", [P, KD, GR], f32r) for n in ("d", "s")]
        ht_lo = [sb(f"a_ht{n}_lo", [P, KD, GR], f32r) for n in ("d", "s")]
        ksb = sb("a_ksb", [P, KD, GR])
        prod = sb("a_prod", [P, KD, GR])
        score = [sb(f"a_score{r}", [H, GR]) for r in range(2)]
        T = ctx.enter_context(nc.psum_tensor("a_T", [P, KD, GR], f32))
        Q = ctx.enter_context(nc.psum_tensor("a_Q", [P, KD, GR], f32))
        K = ctx.enter_context(nc.psum_tensor("a_K", [P, KD, GR], f32))
        V0 = ctx.enter_context(nc.psum_tensor("a_V0", [P, GR], f32))
        S = ctx.enter_context(nc.psum_tensor("a_S", [P, GR], f32))
        V = [V0[:, :], K[:, 0, :]]

        idx_in, idx_set, w_in, bias_in, filled = sem("a_idx_in"), sem("a_idx_set"), sem("a_w_in"), sem("a_bias_in"), sem("a_filled")
        gathered = [[sem(f"a_gathered_{n}{r}") for r in range(4)] for n in ("d", "s")]
        consts, w_split, w_hi_done = sem("a_consts"), sem("a_w_split"), sem("a_w_hi_done")
        stats_done, mv_done, veps_done, rstd_done, nmr_done = (
            sem("a_stats_done"), sem("a_mv_done"), sem("a_veps_done"), sem("a_rstd_done"), sem("a_nmr_done"))
        h_done = [sem("a_hd_done"), sem("a_hs_done")]
        t_done = [sem("a_td_done"), sem("a_ts_done")]
        hi_done = [sem("a_hid_done"), sem("a_his_done")]
        lo_done = [sem("a_lod_done"), sem("a_los_done")]
        q_done, k_done, v_done = sem("a_q_done"), sem("a_k_done"), sem("a_v_done")
        k_out, v_out, prod_done = sem("a_k_out"), sem("a_v_out"), sem("a_prod_done")
        s_done, s_out = sem("a_s_done"), sem("a_s_out")
        stored = [sem(f"a_stored{r}") for r in range(2)]
        passed, pool_passed = sem("a_passed"), sem("a_pool_passed")
        FIRST, LO, HI = -4, 2, 2 + (EG - 6) // 4 * 4
        with nc.Block() as block:
            @block.sync
            def _(sp):
                sp.dma_start(idx[:], ends_cols).then_inc(idx_in, 16)
                for raw, w in zip(w_raw, (wq, wk, wv)):
                    sp.dma_start(raw, w.rearrange("(k p) n -> p k n", p=P)).then_inc(w_in, 16)

                def step(s):
                    if s.exists(EG):
                        sp.wait_ge(s_out, s.times(1, 1))
                        sp.dma_start(score_dram[:, bass.ds(s.times(GR), GR)], score[s.c % 2][:])\
                          .then_inc(stored[s.c % 2], 16)
                pipeline(sp, 0, EG, LO, HI, 4, step)
                for r in range(2):
                    sp.wait_ge(stored[r], 16 * ((EG + 1 - r) // 2))
                sp.wait_ge(filled, 16 * NFILL)

            @block.gpsimd
            def _(pool):
                nc.gpsimd.memset(ident[:], 0.0).then_inc(consts, 1)
                nc.gpsimd.memset(head_of[:], 1.0).then_inc(consts, 1)
                nc.gpsimd.memset(mhalf[:], -0.5).then_inc(consts, 1)
                pool.wait_ge(consts, 3)
                nc.gpsimd.affine_select(out=ident[:], in_=ident[:], compare_op=ALU.not_equal, fill=1.0, base=0,
                                        pattern=[[-1, P]], channel_multiplier=1).then_inc(consts, 1)
                nc.gpsimd.affine_select(out=head_of[:], in_=head_of[:], compare_op=ALU.is_ge, fill=0.0, base=0,
                                        pattern=[[P, KD], [-HD, H]], channel_multiplier=1).then_inc(consts, 1)
                pool.wait_ge(consts, 5)
                nc.gpsimd.affine_select(out=head_of[:], in_=head_of[:], compare_op=ALU.is_ge, fill=0.0, base=HD - 1,
                                        pattern=[[-P, KD], [HD, H]], channel_multiplier=-1).then_inc(consts, 1)
                pool.wait_ge(idx_in, 16)

                def step(s):
                    g = s + 4
                    if g.exists(EG):
                        r = g.c % 4
                        for side in range(2):
                            if g.after(4):
                                pool.wait_ge(h_done[side], g.times(1, -3))
                        nc.gpsimd.tensor_copy(idx_now[g.c % 4][:], idx[:, bass.ds(g.times(2 * GT), 2 * GT)]).then_inc(idx_set, 1)
                        hold(pool, idx_set, g.times(1, 1), pool_passed)
                        for side in range(2):
                            for j in range(GT):
                                nc.gpsimd.indirect_dma_start(
                                    xg[side][r][:, j, :], None, x,
                                    bass.IndirectOffsetOnAxis(idx_now[g.c % 4][:, side * GT + j:side * GT + j + 1], 0),
                                ).then_inc(gathered[side][r], 16)
                    g = s + 2
                    if g.exists(EG):
                        r = g.c % 2
                        hold(pool, mv_done, g.times(1, 1), pool_passed)
                        nc.gpsimd.tensor_scalar(nmean[:, r], mv[:, r, :, :, 0], -1.0, 0.0, ALU.mult, ALU.add)
                        nc.gpsimd.tensor_scalar(veps[:, r], mv[:, r, :, :, 1], 1.0, LN_EPS, ALU.mult, ALU.add)\
                            .then_inc(veps_done, 1)
                        pool.wait_ge(veps_done, g.times(1, 1))
                        nc.gpsimd.tensor_tensor(rstd[:, r], veps[:, r], mhalf[:], ALU.pow).then_inc(rstd_done, 1)
                        pool.wait_ge(rstd_done, g.times(1, 1))
                        nc.gpsimd.tensor_tensor(nmr[:, r], nmean[:, r], rstd[:, r], ALU.mult)\
                            .then_inc(nmr_done, 1)
                pipeline(pool, FIRST, EG, LO, HI, 4, step)

            @block.vector
            def _(dve):
                dve.wait_ge(w_in, 48)
                for n in range(3):
                    nc.vector.tensor_copy(w_hi[n][:], w_raw[n]).then_inc(w_hi_done, 1)
                for n in range(3):
                    dve.wait_ge(w_hi_done, n + 1)
                    nc.vector.tensor_tensor(w_lo[n][:], w_raw[n], w_hi[n][:].bitcast(f32), ALU.subtract)\
                        .then_inc(w_split, 1)

                def step(s):
                    g = s + 2
                    if g.exists(EG):
                        r = g.c % 2
                        if g.after(2):
                            dve.wait_ge(nmr_done, g.times(1, -1))
                        for side in range(2):
                            dve.wait_ge(gathered[side][g.c % 4], g.use(4, 16 * GT))
                            for j in range(GT):
                                nc.vector.bn_stats(stats[:, r, side, j, :], xg[side][g.c % 4][:, j, :]).then_inc(stats_done, 1)
                        for side in range(2):
                            hold(dve, stats_done, g.times(2 * GT, (side + 1) * GT), passed)
                            for j in range(GT):
                                ins = nc.vector.bn_aggr(mv[:, r, side, j, :], stats[:, r, side, j, :])
                        ins.then_inc(mv_done, 1)
                    if s.exists(EG):
                        for c in range(KD):
                            dve.wait_ge(q_done, s.times(KD, c + 1))
                            dve.wait_ge(k_out, s.times(KD, c + 1))
                            if s.after(1):
                                dve.wait_ge(s_done, s.times(1))
                            nc.vector.tensor_tensor(prod[:, c, :], Q[:, c, :], ksb[:, c, :], ALU.mult)\
                                .then_inc(prod_done, 1)
                    g = s + 1
                    if g.exists(EG):
                        for side in range(2):
                            for c in range(KD):
                                dve.wait_ge(hi_done[side], g.times(KD, c + 1))
                                nc.vector.tensor_tensor(ht_lo[side][:, c, :], T[:, c, :],
                                                        ht_hi[side][:, c, :].bitcast(f32), ALU.subtract)\
                                    .then_inc(lo_done[side], 1)
                pipeline(dve, FIRST, EG, LO, HI, 4, step)

            @block.scalar
            def _(act):
                act.dma_start(bias_row[:], wo_b.broadcast_to([P, D])).then_inc(bias_in, 16)
                act.wait_ge(bias_in, 16)
                act.wait_ge(w_split, 3)
                table = agg_dram.rearrange("(n p r) d -> n p r d", n=NFILL, p=P)

                def step(s):
                    if s.exists(EG):
                        for n in range(NFILL // EG):
                            part = table[bass.ds(s.times(NFILL // EG, n), 1)].rearrange("o p r d -> (o p) r d")
                            act.dma_start(part, bias_row[:].rearrange("p (r d) -> p r d", r=1)
                                          .broadcast_to([P, FR, D])).then_inc(filled, 16)
                        for c in range(KD):
                            act.wait_ge(k_done, s.times(KD, c + 1))
                            if s.after(1):
                                act.wait_ge(prod_done, s.times(KD, c - 1))
                            nc.scalar.copy(ksb[:, c, :], K[:, c, :]).then_inc(k_out, 1)
                    g = s + 1

                    def high_part(side):
                        for c in range(KD):
                            act.wait_ge(t_done[side], g.times(1, 1))
                            nc.scalar.copy(ht_hi[side][:, c, :], T[:, c, :]).then_inc(hi_done[side], 1)
                    if g.exists(EG):
                        high_part(0)
                    if s.exists(EG):
                        for c in range(KD):
                            act.wait_ge(v_done, s.times(KD, c + 1))
                            nc.scalar.copy(vt[:, c, bass.ds(s.times(GR), GR)], V[c]).then_inc(v_out, 1)
                    if g.exists(EG):
                        high_part(1)
                    if s.exists(EG):
                        act.wait_ge(s_done, s.times(1, 1))
                        if s.after(2):
                            act.wait_ge(stored[s.c % 2], (s + -2).use(2, 16))
                        nc.scalar.mul(score[s.c % 2][:], S[0:H, :], SCALE).then_inc(s_out, 1)
                    g = s + 2
                    if g.exists(EG):
                        r = g.c % 2
                        act.wait_ge(nmr_done, g.times(1, 1))
                        act.wait_ge(rstd_done, g.times(1, 1))
                        for side in range(2):
                            if g.after(1):
                                act.wait_ge(t_done[side], g.times(1))
                            act.wait_ge(gathered[side][g.c % 4], g.use(4, 16 * GT))
                            for j in range(GT):
                                ins = nc.scalar.activation(h[side][:, j, :], xg[side][g.c % 4][:, j, :], ACT.Relu,
                                                           bias=nmr[:, r, side, j:j + 1], scale=rstd[:, r, side, j:j + 1])
                            ins.then_inc(h_done[side], 1)
                pipeline(act, FIRST, EG, LO, HI, 4, step)

            @block.tensor
            def _(pe):
                pe.wait_ge(consts, 6)
                pe.wait_ge(w_split, 3)

                def project(out, n, side, c):
                    for k in range(KD):
                        for p, (w, a) in enumerate(((w_hi, ht_hi), (w_hi, ht_lo), (w_lo, ht_hi))):
                            ins = nc.tensor.matmul(out, w[n][:, k, c * P:(c + 1) * P], a[side][:, k, :],
                                                   start=(k == 0 and p == 0), stop=(k == KD - 1 and p == 2))
                    return ins

                def transpose(g, side):
                    pe.wait_ge(h_done[side], g.times(1, 1))
                    if side == 1:
                        pe.wait_ge(lo_done[0], g.times(KD, KD))
                    elif g.after(1):
                        pe.wait_ge(lo_done[1], g.times(KD))
                    for j in range(GT):
                        for k in range(KD):
                            ins = nc.tensor.transpose(T[:, k, j * P:(j + 1) * P],
                                                      h[side][:, j, k * P:(k + 1) * P], ident[:])
                    ins.then_inc(t_done[side], 1)

                def step(s):
                    g = s + 1
                    if s.exists(EG):
                        pe.wait_ge(lo_done[0], s.times(KD, KD))
                        if s.after(1):
                            pe.wait_ge(prod_done, s.times(KD))
                        for c in range(KD):
                            project(Q[:, c, :], 0, 0, c).then_inc(q_done, 1)
                        pe.wait_ge(lo_done[1], s.times(KD, KD))
                        if s.after(1):
                            pe.wait_ge(v_out, s.times(KD))
                        for c in range(KD):
                            project(K[:, c, :], 1, 1, c).then_inc(k_done, 1)
                    if g.exists(EG):
                        transpose(g, 0)
                    if s.exists(EG):
                        project(V[0], 2, 1, 0).then_inc(v_done, 1)
                        pe.wait_ge(k_out, s.times(KD, 1))
                        project(V[1], 2, 1, 1).then_inc(v_done, 1)
                    if g.exists(EG):
                        transpose(g, 1)
                    if s.exists(EG):
                        pe.wait_ge(prod_done, s.times(KD, KD))
                        if s.after(1):
                            pe.wait_ge(s_out, s.times(1))
                        for k in range(KD):
                            ins = nc.tensor.matmul(S[0:H, :], head_of[:, k, :], prod[:, k, :],
                                                   start=(k == 0), stop=(k == KD - 1))
                        ins.then_inc(s_done, 1)
                pipeline(pe, FIRST, EG, LO, HI, 4, step)


def softmax_stage(nc, dst_windows, score_dram, alpha_dram, cont_dram):
    with ExitStack() as ctx:
        def sb(name, shape, dt=f32):
            return ctx.enter_context(nc.sbuf_tensor(name, shape, dt))

        def sem(name):
            return ctx.enter_context(nc.semaphore(name))

        dst = sb("b_dst", [P, SE + 2], i32)
        cont = sb("b_cont", [P, SE + 1])
        score, fwd, run = sb("b_score", [P, SE]), sb("b_fwd", [P, SE]), sb("b_run", [P, SE])
        weight = sb("b_weight", [P, SE])
        ident = sb("b_ident", [P, P])
        one = sb("b_one", [1, 1])
        ends = sb("b_ends", [P, 2])
        rows = sb("b_rows", [1, 2, P])
        carry = sb("b_carry", [1, P + 1])
        carry_col = sb("b_carry_col", [P, 1])
        row_ps = ctx.enter_context(nc.psum_tensor("b_row_ps", [P, 2, P], f32))
        col_ps = ctx.enter_context(nc.psum_tensor("b_col_ps", [P, 512], f32))
        loaded, consts, dve_done, rows_done, col_done, exp_done, stored = (
            sem("b_loaded"), sem("b_consts"), sem("b_dve_done"), sem("b_rows_done"), sem("b_col_done"),
            sem("b_exp_done"), sem("b_stored"))
        marks = {}
        with nc.Block() as block:
            @block.gpsimd
            def _(pool):
                nc.gpsimd.memset(ident[:], 0.0).then_inc(consts, 1)
                nc.gpsimd.memset(one[:], 1.0).then_inc(consts, 1)
                pool.wait_ge(consts, 2)
                nc.gpsimd.affine_select(out=ident[:], in_=ident[:], compare_op=ALU.not_equal, fill=1.0, base=0,
                                        pattern=[[-1, P]], channel_multiplier=1).then_inc(consts, 1)

            @block.vector
            def _(dve):
                n = [0]

                def done(ins):
                    n[0] += 1
                    ins.then_inc(dve_done, 1)
                    dve.wait_ge(dve_done, n[0])

                dve.wait_ge(loaded, 32)
                done(nc.vector.tensor_tensor(cont[:], dst[:, 1:SE + 2], dst[:, 0:SE + 1], ALU.is_equal))
                marks["cont"] = n[0]
                done(nc.vector.tensor_reduce(ends[:, 0:1], cont[:, 0:SE], AX.X, ALU.min))
                done(nc.vector.tensor_reduce(ends[:, 1:2], cont[:, 1:SE + 1], AX.X, ALU.min))

                def scan(number, out, values, op, back):
                    turn = slice(None, None, -1) if back else slice(None)
                    flags = (cont[:, 1:SE + 1] if back else cont[:, 0:SE])[:, turn]
                    done(nc.vector.tensor_tensor_scan(out[:, turn], flags, values[:, turn], 0.0, ALU.mult, op))
                    marks["scan", number] = n[0]
                    dve.wait_ge(rows_done, number + 1)
                    done(nc.vector.tensor_copy(rows[:], row_ps[0:1, :, :]))
                    done(nc.vector.memset(carry[:, P:P + 1] if back else carry[:, 0:1], 0.0))
                    to = carry[:, 0:P] if back else carry[:, 1:P + 1]
                    done(nc.vector.tensor_tensor_scan(to[:, turn], rows[:, 1, turn], rows[:, 0, turn], 0.0,
                                                      ALU.mult, op))
                    marks["carry", number] = n[0]
                    dve.wait_ge(col_done, number + 1)
                    done(nc.vector.tensor_copy(carry_col[:], col_ps[:, 0:1]))
                    done(nc.vector.tensor_tensor_scan(out[:, turn], flags, values[:, turn], carry_col[:], ALU.mult, op))

                scan(0, fwd, score, ALU.max, False)
                scan(1, run, fwd, ALU.max, True)
                done(nc.vector.tensor_tensor(score[:], score[:], run[:], ALU.subtract))
                marks["shifted"] = n[0]
                dve.wait_ge(exp_done, 1)
                scan(2, fwd, weight, ALU.add, False)
                scan(3, run, fwd, ALU.max, True)
                done(nc.vector.tensor_scalar(run[:], run[:], SUM_EPS, None, ALU.add))
                done(nc.vector.reciprocal(fwd[:], run[:]))
                done(nc.vector.tensor_tensor(weight[:], weight[:], fwd[:], ALU.mult))
                marks["alpha"] = n[0]

            @block.scalar
            def _(act):
                act.wait_ge(dve_done, marks["shifted"])
                nc.scalar.activation(weight[:], score[:], ACT.Exp).then_inc(exp_done, 1)

            @block.tensor
            def _(pe):
                pe.wait_ge(consts, 3)
                for number, (out, back) in enumerate(((fwd, 0), (run, 1), (fwd, 0), (run, 1))):
                    last = out[:, 0:1] if back else out[:, SE - 1:SE]
                    pe.wait_ge(dve_done, marks["scan", number])
                    nc.tensor.matmul(row_ps[0:1, 0, :], last, ident[:], start=True, stop=True)
                    nc.tensor.matmul(row_ps[0:1, 1, :], ends[:, back:back + 1], ident[:], start=True, stop=True)\
                        .then_inc(rows_done, 1)
                    pe.wait_ge(dve_done, marks["carry", number])
                    nc.tensor.matmul(col_ps[:, 0:1], carry[0:1, back:back + P], one[:], start=True, stop=True)\
                        .then_inc(col_done, 1)

            @block.sync
            def _(sp):
                sp.dma_start(score[:], score_dram.rearrange("h (c e) -> (h c) e", c=SC)).then_inc(loaded, 16)
                sp.dma_start(dst[:], dst_windows).then_inc(loaded, 16)
                sp.wait_ge(dve_done, marks["cont"])
                sp.dma_start(cont_dram.rearrange("o (c e) -> (o c) e", c=SC), cont[0:SC, 0:SE]).then_inc(stored, 16)
                sp.wait_ge(dve_done, marks["alpha"])
                sp.dma_start(alpha_dram.rearrange("h (c e) -> (h c) e", c=SC), weight[:]).then_inc(stored, 16)
                sp.wait_ge(stored, 32)


def message_stage(nc, dst_cols, next_cols, wo, wo_b, vt, alpha_dram, cont_dram, agg_dram):
    with ExitStack() as ctx:
        def sb(name, shape, dt=f32):
            return ctx.enter_context(nc.sbuf_tensor(name, shape, dt))

        def sem(name):
            return ctx.enter_context(nc.semaphore(name))

        spread = sb("c_spread", [H, KD, P])
        dst, nxt = sb("c_dst", [P, EG * GT], i32), sb("c_next", [P, EG * GT], i32)
        same, row_of = sb("c_same", [P, EG * GT]), sb("c_row_of", [P, EG * GT], i32)
        row_now = [sb(f"c_row_now{r}", [P, GT], i32) for r in range(2)]
        w = sb("c_wo", [P, KD, D])
        bias_row = sb("c_bias_row", [P, D])
        alpha = [sb(f"c_alpha{r}", [H, GR]) for r in range(2)]
        cont = [sb(f"c_cont{r}", [P, GR]) for r in range(2)]
        msg = [sb(f"c_msg{r}", [P, KD, GR]) for r in range(2)]
        total = [sb(f"c_total{r}", [P, KD, GR]) for r in range(2)]
        rows = [sb(f"c_rows{r}", [P, GT, D]) for r in range(2)]
        A = [ctx.enter_context(nc.psum_tensor(f"c_A{r}", [P, KD, GR], f32)) for r in range(2)]
        Y = [ctx.enter_context(nc.psum_tensor(f"c_Y{r}", [P, GT, D], f32)) for r in range(2)]
        loaded, consts, same_done, index_done = sem("c_loaded"), sem("c_consts"), sem("c_same_done"), sem("c_index_done")
        group_in = [sem(f"c_group_in{r}") for r in range(2)]
        a_done, msg_done, total_done, y_done, rows_done = (
            sem("c_a_done"), sem("c_msg_done"), sem("c_total_done"), sem("c_y_done"), sem("c_rows_done"))
        scattered = [sem(f"c_scattered{r}") for r in range(2)]
        row_set, passed = sem("c_row_set"), sem("c_passed")
        FIRST, LO, HI = -1, 3, EG - 2
        with nc.Block() as block:
            @block.sync
            def _(sp):
                sp.dma_start(dst[:], dst_cols).then_inc(loaded, 16)
                sp.dma_start(nxt[:], next_cols).then_inc(loaded, 16)
                sp.dma_start(w[:], wo.rearrange("(k p) n -> p k n", p=P)).then_inc(loaded, 16)
                sp.dma_start(bias_row[:], wo_b.broadcast_to([P, D])).then_inc(loaded, 16)

                def step(s):
                    g = s + 1
                    if g.exists(EG):
                        r = g.c % 2
                        if g.after(2):
                            sp.wait_ge(total_done, g.times(KD, -KD))
                        sp.dma_start(alpha[r][:], alpha_dram[:, bass.ds(g.times(GR), GR)]).then_inc(group_in[r], 16)
                        sp.dma_start(cont[r][:], cont_dram[:, bass.ds(g.times(GR), GR)].broadcast_to([P, GR]))\
                          .then_inc(group_in[r], 16)
                pipeline(sp, FIRST, EG, LO, HI, 2, step)

            @block.tensor
            def _(pe):
                pe.wait_ge(consts, 3)
                pe.wait_ge(loaded, 64)

                def step(s):
                    g = s + 1
                    if g.exists(EG):
                        r = g.c % 2
                        pe.wait_ge(group_in[r], g.use(2, 32))
                        if g.after(2):
                            pe.wait_ge(msg_done, g.times(KD, -KD))
                        for c in range(KD):
                            nc.tensor.matmul(A[r][:, c, :], spread[:, c, :], alpha[r][:], start=True, stop=True)\
                                .then_inc(a_done, 1)
                    if s.exists(EG):
                        r = s.c % 2
                        pe.wait_ge(total_done, s.times(KD, KD))
                        if s.after(2):
                            pe.wait_ge(rows_done, s.times(1, -1))
                        for j in range(GT):
                            for k in range(KD):
                                ins = nc.tensor.matmul(Y[r][:, j, :], total[r][:, k, j * P:(j + 1) * P], w[:, k, :],
                                                       start=(k == 0), stop=(k == KD - 1))
                        ins.then_inc(y_done, 1)
                pipeline(pe, FIRST, EG, LO, HI, 2, step)

            @block.vector
            def _(dve):
                dve.wait_ge(loaded, 64)
                nc.vector.tensor_tensor(same[:], dst[:], nxt[:], ALU.is_equal).then_inc(same_done, 1)
                dve.wait_ge(same_done, 1)
                nc.vector.scalar_tensor_tensor(row_of[:], same[:], float(SKIP), dst[:], ALU.mult, ALU.add)\
                    .then_inc(index_done, 1)

                def step(s):
                    if s.exists(EG):
                        r = s.c % 2
                        dve.wait_ge(group_in[r], s.use(2, 32))
                        if s.after(2):
                            dve.wait_ge(y_done, s.times(1, -1))
                        for c in range(KD):
                            dve.wait_ge(a_done, s.times(KD, c + 1))
                            nc.vector.tensor_tensor(msg[r][:, c, :], A[r][:, c, :],
                                                    vt[:, c, bass.ds(s.times(GR), GR)], ALU.mult).then_inc(msg_done, 1)
                        for c in range(KD):
                            dve.wait_ge(msg_done, s.times(KD, c + 1))
                            if s.after(1):
                                dve.wait_ge(total_done, s.times(KD, c - 1))
                            before = total[1 - r][:, c, GR - 1:GR] if s.after(1) else 0.0
                            nc.vector.tensor_tensor_scan(total[r][:, c, :], cont[r][:], msg[r][:, c, :], before,
                                                         ALU.mult, ALU.add).then_inc(total_done, 1)
                    g = s + -1
                    if g.exists(EG):
                        r = g.c % 2
                        dve.wait_ge(y_done, g.times(1, 1))
                        if g.after(2):
                            dve.wait_ge(scattered[r], (g + -2).use(2, 16 * GT))
                        nc.vector.tensor_tensor(rows[r][:], Y[r][:], bias_row[:].rearrange("p (j d) -> p j d", j=1)
                                                .broadcast_to([P, GT, D]), ALU.add).then_inc(rows_done, 1)
                pipeline(dve, 0, EG + 1, LO, HI, 2, step)

            @block.gpsimd
            def _(pool):
                nc.gpsimd.memset(spread[:], 1.0).then_inc(consts, 1)
                pool.wait_ge(consts, 1)
                nc.gpsimd.affine_select(out=spread[:], in_=spread[:], compare_op=ALU.is_ge, fill=0.0, base=0,
                                        pattern=[[P, KD], [1, P]], channel_multiplier=-HD).then_inc(consts, 1)
                pool.wait_ge(consts, 2)
                nc.gpsimd.affine_select(out=spread[:], in_=spread[:], compare_op=ALU.is_ge, fill=0.0, base=HD - 1,
                                        pattern=[[-P, KD], [-1, P]], channel_multiplier=HD).then_inc(consts, 1)
                pool.wait_ge(index_done, 1)

                def step(s):
                    if s.exists(EG):
                        r = s.c % 2
                        pool.wait_ge(rows_done, s.times(1, 1))
                        nc.gpsimd.tensor_copy(row_now[r][:], row_of[:, bass.ds(s.times(GT), GT)]).then_inc(row_set, 1)
                        hold(pool, row_set, s.times(1, 1), passed)
                        for j in range(GT):
                            nc.gpsimd.indirect_dma_start(
                                agg_dram, bass.IndirectOffsetOnAxis(row_now[r][:, j:j + 1], 0),
                                rows[r][:, j, :], None, bounds_check=N - 1, oob_is_err=False,
                            ).then_inc(scattered[r], 16)
                pipeline(pool, 0, EG, LO, HI, 2, step)
                for r in range(2):
                    pool.wait_ge(scattered[r], 16 * GT * ((EG + 1 - r) // 2))


def node_stage(nc, x, given, w1, w2, out, agg_dram):
    with ExitStack() as ctx:
        def sb(name, shape, dt=f32):
            return ctx.enter_context(nc.sbuf_tensor(name, shape, dt))

        def sem(name):
            return ctx.enter_context(nc.semaphore(name))

        def psum(name, shape):
            return ctx.enter_context(nc.psum_tensor(name, shape, f32))

        w1_raw, w2_raw = sb("d_w1_raw", [P, KD, F]), sb("d_w2_raw", [P, KF, D])
        w1_hi, w1_lo = sb("d_w1_hi", [P, KD, F], f32r), sb("d_w1_lo", [P, KD, F], f32r)
        w2_hi, w2_lo = sb("d_w2_hi", [P, KF, D], f32r), sb("d_w2_lo", [P, KF, D], f32r)
        g1_col, b1_col, fb1_col = sb("d_g1_col", [P, KD]), sb("d_b1_col", [P, KD]), sb("d_fb1_col", [P, KF])
        g2_row, b2_row = sb("d_g2_row", [P, D]), sb("d_b2_row", [P, D])
        res_col = sb("d_res_col", [P, KD])
        ident = sb("d_ident", [P, P])
        mhalf = sb("d_mhalf", [P, GT])
        xt = [sb(f"d_x{r}", [P, GT, D]) for r in range(4)]
        xb = [sb(f"d_xb{r}", [P, GT, D]) for r in range(4)]
        agg = [sb(f"d_agg{r}", [P, GT, D]) for r in range(2)]
        h = [sb(f"d_h{r}", [P, GT, D]) for r in range(2)]
        z = sb("d_z", [P, GT, D])
        zn = [sb(f"d_zn{r}", [P, GT, D]) for r in range(2)]
        zt_hi, zt_lo = sb("d_zt_hi", [P, KD, GR], f32r), sb("d_zt_lo", [P, KD, GR], f32r)
        act_full = sb("d_act", [P, KF, GR])
        act_hi, act_lo = sb("d_act_hi", [P, KF, GR], f32r), sb("d_act_lo", [P, KF, GR], f32r)
        ut = sb("d_ut", [P, KD, GR])
        yn = sb("d_yn", [P, GT, D])
        o = [sb(f"d_o{r}", [P, GT, D]) for r in range(2)]
        norm = {n: dict(stats=sb(f"d_stats_{n}", [P, 2, GT, 6]), mv=sb(f"d_mv_{n}", [P, 2, GT, 2]),
                        veps=sb(f"d_veps_{n}", [P, 2, GT]), rstd=sb(f"d_rstd_{n}", [P, 2, GT]),
                        nmean=sb(f"d_nmean_{n}", [P, 2, GT]), nmr=sb(f"d_nmr_{n}", [P, 2, GT]), stats_done=sem(f"d_stats_done_{n}"),
                        mv_done=sem(f"d_mv_done_{n}"), veps_done=sem(f"d_veps_done_{n}"),
                        rstd_done=sem(f"d_rstd_done_{n}"), nmr_done=sem(f"d_nmr_done_{n}")) for n in "xzy"}
        T, FF = psum("d_T", [P, KD, GR]), psum("d_F", [P, 2, GR])
        Y = [psum(f"d_Y{r}", [P, GT, D]) for r in range(2)]

        w_in, consts, prep, bias_ps = sem("d_w_in"), sem("d_consts"), sem("d_prep"), sem("d_bias_ps")
        x_in = [sem(f"d_x_in{r}") for r in range(4)]
        agg_in = [sem(f"d_agg_in{r}") for r in range(2)]
        stored = [sem(f"d_stored{r}") for r in range(2)]
        h_done, z_done, zn_done, xb_done = sem("d_h_done"), sem("d_z_done"), sem("d_zn_done"), sem("d_xb_done")
        t_done, hi_done, lo_done = sem("d_t_done"), sem("d_hi_done"), sem("d_lo_done")
        f_done, gelu_done, ghi_done, ghi_last, glo_done = (
            sem("d_f_done"), sem("d_gelu_done"), sem("d_ghi_done"), sem("d_ghi_last"), sem("d_glo_done"))
        ut_done = sem("d_ut_done")
        ffn_done, yn_done, scaled, o_done = sem("d_ffn_done"), sem("d_yn_done"), sem("d_scaled"), sem("d_o_done")
        passed, pool_passed = sem("d_passed"), sem("d_pool_passed")
        v = given
        vectors = ((g1_col, v["g1_col"]), (b1_col, v["b1_col"]), (fb1_col, v["fb1_col"]),
                   (g2_row, v["g2"].broadcast_to([P, D])),
                   (b2_row, v["b2"].broadcast_to([P, D])),
                   (res_col, v["fb2_col"]))
        N_IN = 16 * (2 + len(vectors))
        FIRST, LO, HI, LAST = -4, 5, NG - 5, NG + 2
        PREP = 8

        def wide(row):
            return row[:].rearrange("p (j d) -> p j d", j=1).broadcast_to([P, GT, D])

        def rows_of(table, g):
            at = g.times(GR) if g.i is not None or g.c < NG - 1 else N - GR
            return table[bass.ds(at, GR), :].rearrange("(p j) d -> p j d", j=GT)

        with nc.Block() as block:
            @block.sync
            def _(sp):
                sp.dma_start(w1_raw[:], w1.rearrange("(k p) n -> p k n", p=P)).then_inc(w_in, 16)
                sp.dma_start(w2_raw[:], w2.rearrange("(k p) n -> p k n", p=P)).then_inc(w_in, 16)
                for to, of in vectors:
                    sp.dma_start(to[:], of).then_inc(w_in, 16)

                def step(s):
                    g = s + 4
                    if g.exists(NG):
                        if g.after(4):
                            sp.wait_ge(xb_done, g.times(1, -3))
                            sp.wait_ge(h_done, g.times(1, -3))
                        sp.dma_start(xt[g.c % 4][:], rows_of(x, g)).then_inc(x_in[g.c % 4], 16)
                    g = s + 3
                    if g.exists(NG):
                        if g.after(2):
                            sp.wait_ge(z_done, g.times(1, -1))
                        sp.dma_start(agg[g.c % 2][:], rows_of(agg_dram, g)).then_inc(agg_in[g.c % 2], 16)
                    g = s + -2
                    if g.exists(NG):
                        sp.wait_ge(o_done, g.times(1, 1))
                        if g.i is None and g.c == NG - 1:
                            sp.wait_ge(stored[(g.c - 1) % 2], (g + -1).use(2, 16))
                        sp.dma_start(rows_of(out, g), o[g.c % 2][:]).then_inc(stored[g.c % 2], 16)
                pipeline(sp, FIRST, LAST, LO, HI, 4, step)
                for r in range(2):
                    sp.wait_ge(stored[r], 16 * ((NG + 1 - r) // 2))

            @block.gpsimd
            def _(pool):
                nc.gpsimd.memset(ident[:], 0.0).then_inc(consts, 1)
                nc.gpsimd.memset(mhalf[:], -0.5).then_inc(consts, 1)
                pool.wait_ge(consts, 2)
                nc.gpsimd.affine_select(out=ident[:], in_=ident[:], compare_op=ALU.not_equal, fill=1.0, base=0,
                                        pattern=[[-1, P]], channel_multiplier=1).then_inc(consts, 1)
                pool.wait_ge(w_in, N_IN)

                def scales(n, g):
                    q, r = norm[n], g.c % 2
                    hold(pool, q["mv_done"], g.times(1, 1), pool_passed)
                    nc.gpsimd.tensor_scalar(q["nmean"][:, r], q["mv"][:, r, :, 0], -1.0, 0.0, ALU.mult, ALU.add)
                    nc.gpsimd.tensor_scalar(q["veps"][:, r], q["mv"][:, r, :, 1], 1.0, LN_EPS, ALU.mult, ALU.add)\
                        .then_inc(q["veps_done"], 1)
                    pool.wait_ge(q["veps_done"], g.times(1, 1))
                    nc.gpsimd.tensor_tensor(q["rstd"][:, r], q["veps"][:, r], mhalf[:], ALU.pow)\
                        .then_inc(q["rstd_done"], 1)
                    pool.wait_ge(q["rstd_done"], g.times(1, 1))
                    nc.gpsimd.tensor_tensor(q["nmr"][:, r], q["nmean"][:, r], q["rstd"][:, r], ALU.mult)\
                        .then_inc(q["nmr_done"], 1)

                def step(s):
                    g = s + -2
                    if g.exists(NG):
                        pool.wait_ge(yn_done, g.times(1, 1))
                        if g.after(2):
                            pool.wait_ge(stored[g.c % 2], (g + -2).use(2, 16))
                        nc.gpsimd.tensor_tensor(o[g.c % 2][:], yn[:], wide(g2_row), ALU.mult).then_inc(scaled, 1)
                    g = s + -1
                    if g.exists(NG):
                        scales("y", g)
                    g = s + 3
                    if g.exists(NG):
                        scales("x", g)
                    g = s + 1
                    if g.exists(NG):
                        pool.wait_ge(x_in[g.c % 4], g.use(4, 16))
                        if g.after(4):
                            pool.wait_ge(o_done, g.times(1, -3))
                        nc.gpsimd.tensor_tensor(xb[g.c % 4][:], xt[g.c % 4][:], wide(b2_row), ALU.add)\
                            .then_inc(xb_done, 1)
                    g = s + 2
                    if g.exists(NG):
                        scales("z", g)
                pipeline(pool, FIRST, LAST, LO, HI, 4, step)

            @block.vector
            def _(dve):
                n = [0]

                def done(ins):
                    n[0] += 1
                    ins.then_inc(prep, 1)
                    dve.wait_ge(prep, n[0])

                dve.wait_ge(w_in, N_IN)
                dve.wait_ge(bias_ps, 1)
                done(nc.vector.tensor_tensor(fb1_col[:], fb1_col[:], FF[:, 0, 0:KF], ALU.add))
                for k in range(KD):
                    done(nc.vector.tensor_scalar(w1_raw[:, k, :], w1_raw[:, k, :], g1_col[:, k:k + 1], None, ALU.mult))
                done(nc.vector.tensor_copy(w1_hi[:], w1_raw[:]))
                done(nc.vector.tensor_tensor(w1_lo[:], w1_raw[:], w1_hi[:].bitcast(f32), ALU.subtract))
                done(nc.vector.tensor_copy(w2_hi[:], w2_raw[:]))
                done(nc.vector.tensor_tensor(w2_lo[:], w2_raw[:], w2_hi[:].bitcast(f32), ALU.subtract))
                done(nc.vector.tensor_tensor(res_col[:], res_col[:], b1_col[:], ALU.add))

                def statistics(name, g, t):
                    q, r = norm[name], g.c % 2
                    for j in range(GT):
                        nc.vector.bn_stats(q["stats"][:, r, j, :], t[:, j, :]).then_inc(q["stats_done"], 1)
                    hold(dve, q["stats_done"], g.times(GT, GT), passed)
                    for j in range(GT):
                        ins = nc.vector.bn_aggr(q["mv"][:, r, j, :], q["stats"][:, r, j, :])
                    ins.then_inc(q["mv_done"], 1)

                def low_part(s, c):
                    if c < KF - 1:
                        dve.wait_ge(ghi_done, s.times(KF - 1, c + 1))
                    else:
                        dve.wait_ge(gelu_done, s.times(KF, KF))
                        nc.vector.tensor_copy(act_hi[:, c, :], act_full[:, c, :]).then_inc(ghi_last, 1)
                        dve.wait_ge(ghi_last, s.times(1, 1))
                    nc.vector.tensor_tensor(act_lo[:, c, :], act_full[:, c, :], act_hi[:, c, :].bitcast(f32),
                                            ALU.subtract).then_inc(glo_done, 1)

                def step(s):
                    g = s + -1
                    if g.exists(NG):
                        dve.wait_ge(ffn_done, g.times(1, 1))
                        statistics("y", g, Y[g.c % 2])
                    if s.exists(NG):
                        low_part(s, 0)
                    g = s + 3
                    if g.exists(NG):
                        dve.wait_ge(x_in[g.c % 4], g.use(4, 16))
                        statistics("x", g, xt[g.c % 4])
                    if s.exists(NG):
                        low_part(s, 1)
                    g = s + 2
                    if g.exists(NG):
                        r = g.c % 2
                        dve.wait_ge(h_done, g.times(1, 1))
                        dve.wait_ge(agg_in[r], g.use(2, 16))
                        if g.after(1):
                            dve.wait_ge(zn_done, g.times(1))
                        nc.vector.tensor_tensor(z[:], h[r][:], agg[r][:], ALU.add).then_inc(z_done, 1)
                    if s.exists(NG):
                        low_part(s, 2)
                    if g.exists(NG):
                        dve.wait_ge(z_done, g.times(1, 1))
                        statistics("z", g, z)
                    if s.exists(NG):
                        low_part(s, 3)
                    g = s + 1
                    if g.exists(NG):
                        dve.wait_ge(hi_done, g.times(1, 1))
                        nc.vector.tensor_tensor(zt_lo[:], T[:], zt_hi[:].bitcast(f32), ALU.subtract).then_inc(lo_done, 1)
                    g = s + -2
                    if g.exists(NG):
                        r = g.c % 2
                        dve.wait_ge(scaled, g.times(1, 1))
                        dve.wait_ge(xb_done, g.times(1, 1))
                        nc.vector.tensor_tensor(o[r][:], o[r][:], xb[g.c % 4][:], ALU.add).then_inc(o_done, 1)
                pipeline(dve, FIRST, LAST, LO, HI, 4, step)

            @block.scalar
            def _(act):
                act.wait_ge(prep, PREP)

                def normalize(name, g, to, of, j, func=ACT.Identity):
                    q, r = norm[name], g.c % 2
                    return nc.scalar.activation(to[:, j, :], of[:, j, :], func, bias=q["nmr"][:, r, j:j + 1],
                                                scale=q["rstd"][:, r, j:j + 1])

                def gelu(s, c):
                    act.wait_ge(f_done, s.times(KF, c + 1))
                    if s.after(1):
                        act.wait_ge(glo_done, s.times(KF, c + 1 - KF))
                    nc.scalar.activation(act_full[:, c, :], FF[:, c % 2, :], ACT.Gelu, bias=fb1_col[:, c:c + 1])\
                        .then_inc(gelu_done, 1)
                    if c == KF - 1:
                        return
                    act.wait_ge(gelu_done, s.times(KF, c + 1))
                    nc.scalar.activation(act_hi[:, c, :], act_full[:, c, :], ACT.Identity).then_inc(ghi_done, 1)

                def step(s):
                    g = s + 1
                    r = g.c % 2

                    def norm_z(tiles):
                        if g.exists(NG):
                            if 0 in tiles:
                                act.wait_ge(norm["z"]["nmr_done"], g.times(1, 1))
                                if g.after(2):
                                    act.wait_ge(t_done, g.times(1, -1))
                            for j in tiles:
                                ins = normalize("z", g, zn[r], z, j)
                            if GT - 1 in tiles:
                                ins.then_inc(zn_done, 1)
                    norm_z((0, 1))
                    if s.exists(NG):
                        gelu(s, 0)
                    norm_z((2,))
                    if s.exists(NG):
                        gelu(s, 1)
                    norm_z((3,))
                    if s.exists(NG):
                        gelu(s, 2)
                        gelu(s, 3)
                    g2 = s + -1
                    if g2.exists(NG):
                        act.wait_ge(norm["y"]["nmr_done"], g2.times(1, 1))
                        if g2.after(1):
                            act.wait_ge(scaled, g2.times(1))
                        for j in range(GT // 2):
                            normalize("y", g2, yn, Y[g2.c % 2], j)
                    if g.exists(NG):
                        act.wait_ge(t_done, g.times(1, 1))
                        nc.scalar.activation(zt_hi[:], T[:], ACT.Identity).then_inc(hi_done, 1)
                    if g2.exists(NG):
                        for j in range(GT // 2, GT):
                            ins = normalize("y", g2, yn, Y[g2.c % 2], j)
                        ins.then_inc(yn_done, 1)
                    g3 = s + 3
                    if g3.exists(NG):
                        act.wait_ge(norm["x"]["nmr_done"], g3.times(1, 1))
                        if g3.after(2):
                            act.wait_ge(z_done, g3.times(1, -1))
                        for j in range(GT):
                            ins = normalize("x", g3, h[g3.c % 2], xt[g3.c % 4], j, ACT.Relu)
                        ins.then_inc(h_done, 1)
                    if g.exists(NG):
                        act.wait_ge(lo_done, g.times(1, 1))
                        for k in range(KD):
                            nc.scalar.activation(ut[:, k, :], T[:, k, :], ACT.Identity, bias=res_col[:, k:k + 1],
                                                 scale=g1_col[:, k:k + 1]).then_inc(ut_done, 1)
                pipeline(act, FIRST, LAST, LO, HI, 4, step)

            @block.tensor
            def _(pe):
                pe.wait_ge(w_in, N_IN)
                for c in range(KF):
                    for k in range(KD):
                        ins = nc.tensor.matmul(FF[:, 0, c:c + 1], w1_raw[:, k, c * P:(c + 1) * P], b1_col[:, k:k + 1],
                                               start=(k == 0), stop=(k == KD - 1))
                ins.then_inc(bias_ps, 1)
                pe.wait_ge(consts, 3)
                pe.wait_ge(prep, PREP)

                def step(s):
                    out = Y[s.c % 2]
                    if s.exists(NG):
                        pe.wait_ge(lo_done, s.times(1, 1))
                        for c in range(KF):
                            if s.after(1) or c >= 2:
                                pe.wait_ge(gelu_done, s.times(KF, c - 1))
                            for k in range(KD):
                                for p, (w, a) in enumerate(((w1_hi, zt_hi), (w1_hi, zt_lo), (w1_lo, zt_hi))):
                                    ins = nc.tensor.matmul(FF[:, c % 2, :], w[:, k, c * P:(c + 1) * P], a[:, k, :],
                                                           start=(k == 0 and p == 0), stop=(k == KD - 1 and p == 2))
                            ins.then_inc(f_done, 1)
                        if s.after(2):
                            pe.wait_ge(yn_done, s.times(1, -1))
                        pe.wait_ge(ut_done, s.times(KD, KD))
                        for j in range(GT):
                            for k in range(KD):
                                nc.tensor.matmul(out[:, j, k * P:(k + 1) * P], ut[:, k, j * P:(j + 1) * P], ident[:],
                                                 is_transpose=True, start=(j % 2 == 0 and k == 0), stop=False,
                                                 skip_group_check=True)
                    g = s + 1
                    if g.exists(NG):
                        pe.wait_ge(zn_done, g.times(1, 1))
                        if g.after(1):
                            pe.wait_ge(lo_done, g.times(1))
                            pe.wait_ge(ut_done, g.times(KD))
                        for j in range(GT):
                            for k in range(KD):
                                ins = nc.tensor.transpose(T[:, k, j * P:(j + 1) * P],
                                                          zn[g.c % 2][:, j, k * P:(k + 1) * P], ident[:])
                        ins.then_inc(t_done, 1)
                    if s.exists(NG):
                        for c in range(KF):
                            pe.wait_ge(glo_done, s.times(KF, c + 1))
                            for j in range(GT):
                                for a, w in ((act_hi, w2_hi), (act_lo, w2_hi), (act_hi, w2_lo)):
                                    ins = nc.tensor.matmul(out[:, j, :], a[:, c, j * P:(j + 1) * P], w[:, c, :],
                                                           start=False, stop=(c == KF - 1 and w is w2_lo),
                                                           skip_group_check=True)
                        ins.then_inc(ffn_done, 1)
                pipeline(pe, FIRST, LAST, LO, HI, 4, step)


def program(nc, x, ends_cols, dst_row_cols, next_cols, dst_windows, wq, wk, wv, wo, wo_b, g2, b2,
            g1_col, b1_col, fb1_col, fb2_col, w1, w2, out):
    with ExitStack() as ctx:
        score_dram = nc.dram_tensor("score_scratch", [H, EP], f32).ap()
        alpha_dram = nc.dram_tensor("alpha_scratch", [H, EP], f32).ap()
        cont_dram = nc.dram_tensor("cont_scratch", [1, EP], f32).ap()
        agg_dram = nc.dram_tensor("agg_scratch", [NP, D], f32).ap()
        with nc.sbuf_tensor("vt", [P, KD, EP], f32) as vt:
            score_stage(nc, x, ends_cols, wq, wk, wv, wo_b, vt, score_dram, agg_dram)
            softmax_stage(nc, dst_windows, score_dram, alpha_dram, cont_dram)
            message_stage(nc, dst_row_cols, next_cols, wo, wo_b, vt, alpha_dram, cont_dram, agg_dram)
        vectors = dict(g2=g2, b2=b2, g1_col=g1_col, b1_col=b1_col, fb1_col=fb1_col, fb2_col=fb2_col)
        node_stage(nc, x, vectors, w1, w2, out, agg_dram)


def kernel(**inputs):
    import numpy as _np
    import concourse.bacc as _bacc
    from concourse import mybir as _mybir
    from concourse.bass_utils import run_bass_kernel_spmd as _run

    given = {k: _np.asarray(v) for k, v in inputs.items()}
    src, dst = given["src"], given["dst"]

    def columns(a, fill):
        padded = _np.full(EP, fill, a.dtype)
        padded[:E] = a
        return padded.reshape(EG, GT, P).transpose(2, 0, 1)

    ext = _np.full(EP + 2, N, dst.dtype)
    ext[0], ext[-1] = -1, N + 1
    ext[1:E + 1] = dst
    windows = _np.stack([ext[c * SE:c * SE + SE + 2] for c in range(SC)])
    L = "L0_gnn_"
    arrays = dict(
        x=given["x"], ends_cols=_np.stack([columns(dst, 0), columns(src, 0)], axis=2).reshape(P, -1),
        dst_row_cols=_np.ascontiguousarray(ext[1:-1].reshape(EG * GT, P).T),
        next_cols=_np.ascontiguousarray(ext[2:].reshape(EG * GT, P).T),
        dst_windows=_np.ascontiguousarray(_np.concatenate([windows] * H)),
        wq=given[L + "Wq"], wk=given[L + "Wk"], wv=given[L + "Wv"], wo=given[L + "Wo_w"],
        wo_b=given[L + "Wo_b"].reshape(1, D), 
        g2=given[L + "ln2_g"].reshape(1, D), b2=given[L + "ln2_b"].reshape(1, D),
        g1_col=_np.ascontiguousarray(given[L + "ln1_g"].reshape(KD, P).T),
        b1_col=_np.ascontiguousarray(given[L + "ln1_b"].reshape(KD, P).T),
        fb1_col=_np.ascontiguousarray(given[L + "ffn_b1"].reshape(KF, P).T),
        fb2_col=_np.ascontiguousarray(given[L + "ffn_b2"].reshape(KD, P).T), w1=given[L + "ffn_w1"], w2=given[L + "ffn_w2"])
    nc = _bacc.Bacc("TRN2", target_bir_lowering=False, num_devices=1)
    args, host = {}, {}
    for name, a in arrays.items():
        a = _np.ascontiguousarray(a)
        host[f"in_{name}"] = a
        args[name] = nc.dram_tensor(f"in_{name}", a.shape, _mybir.dt.from_np(a.dtype), kind="ExternalInput").ap()
    args["out"] = nc.dram_tensor("out_0", (N, D), _mybir.dt.float32, kind="ExternalOutput").ap()
    program(nc, **args)
    r = _run(nc, [host], core_ids=[0])
    return r.results[0]["out_0"]
```
